# Optimizing a Trainium2 kernel written in Bass

```python
import numpy as np
import jax
import jax.numpy as jnp

def _softmax(x, axis=-1):
    return jax.nn.softmax(x, axis=axis)

def _gelu(x):
    return jax.nn.gelu(x, approximate=True)

def _silu(x):
    return jax.nn.silu(x)

def _sigmoid(x):
    return jax.nn.sigmoid(x)

def _layernorm(x, axis=-1, eps=1e-05):
    m = jnp.mean(x, axis=axis, keepdims=True)
    v = jnp.var(x, axis=axis, keepdims=True)
    return (x - m) / jnp.sqrt(v + eps)

def _scatter_add(tgt, idx, src, axis=0):
    return tgt.at[idx].add(src)

def _segment_sum(src, seg, n):
    return jax.ops.segment_sum(src, seg, n)
kernel_name = 'mk_gnn_preln_d2_gnn_r8_6061e9'

def setup_inputs(seed: int=0):
    np.random.seed(seed)
    _w = jnp.asarray

    def _rec_inputs():
        import jax
        import jax.numpy as jnp
        _gk = jax.random.key(seed)
        x = -0.000202 + 1 * jax.random.normal(jax.random.fold_in(_gk, 1), (6250, 128), jnp.float32)
        _s = jax.random.randint(jax.random.fold_in(_gk, 2), (50000,), 0, 6250, jnp.int32)
        _d = jax.random.randint(jax.random.fold_in(_gk, 3), (50000,), 0, 6250, jnp.int32)
        _loop = jnp.arange(6250, dtype=jnp.int32)
        src = jnp.concatenate([_s, _d, _loop])
        dst = jnp.concatenate([_d, _s, _loop])
        _o = jnp.argsort(dst, stable=True)
        src = src[_o]
        dst = dst[_o]
        edge_attr_16 = 0.000254156 + 0.999948 * jax.random.normal(jax.random.fold_in(_gk, 13), (106250, 16), jnp.float32)
        edge_attr_32 = -5.3897e-05 + 0.999841 * jax.random.normal(jax.random.fold_in(_gk, 14), (106250, 32), jnp.float32)
        return (x, src, dst, edge_attr_16, edge_attr_32)
    x, src, dst, edge_attr_16, edge_attr_32 = _rec_inputs()

    def _L0_gnn_setup():
        import jax, jax.numpy as jnp
        import numpy as np
        N_NODES = 6250
        N_EDGES = 100000
        IN_FEATS = 128
        HEADS = 4
        OUT_FEATS = 32
        NEG_SLOPE = 0.2

        def _edge_softmax(e, dst, n_nodes):
            seg_max = jax.ops.segment_max(e, dst, num_segments=n_nodes)
            ex = jnp.exp(e - seg_max[dst])
            seg_sum = jax.ops.segment_sum(ex, dst, num_segments=n_nodes)
            return ex / seg_sum[dst]
        key = jax.random.key(seed)
        ks = jax.random.split(key, 9)
        HD = HEADS * OUT_FEATS
        return {'feat': jax.random.normal(ks[0], (N_NODES, IN_FEATS), dtype=jnp.float32), 'W_src': jax.random.normal(ks[1], (HD, IN_FEATS), dtype=jnp.float32) * (1.0 / np.sqrt(IN_FEATS)), 'b_src': jax.random.normal(ks[2], (HD,), dtype=jnp.float32) * 0.02, 'W_dst': jax.random.normal(ks[3], (HD, IN_FEATS), dtype=jnp.float32) * (1.0 / np.sqrt(IN_FEATS)), 'b_dst': jax.random.normal(ks[4], (HD,), dtype=jnp.float32) * 0.02, 'W_v': jax.random.normal(ks[5], (HD, IN_FEATS), dtype=jnp.float32) * (1.0 / np.sqrt(IN_FEATS)), 'b_v': jax.random.normal(ks[6], (HD,), dtype=jnp.float32) * 0.02, 'src': jax.random.randint(ks[7], (N_EDGES,), 0, N_NODES, dtype=jnp.int32), 'dst': jax.random.randint(ks[8], (N_EDGES,), 0, N_NODES, dtype=jnp.int32)}
    _L0_gnn_all = _L0_gnn_setup()
    _L0_gnn_in = {k: v for k, v in _L0_gnn_all.items() if k in ('W_src', 'b_src', 'W_dst', 'b_dst', 'W_v', 'b_v')}
    del _L0_gnn_all

    def _L1_gnn_setup():
        import jax, jax.numpy as jnp
        import numpy as np
        N, E, D, SD, SH, EA, FC, H = (6250, 100000, 128, 64, 16, 32, 128, 8)
        EPS = 1e-05
        key = jax.random.key(seed)
        ks = jax.random.split(key, 20)
        rn = lambda k, shp, fan: jax.random.normal(k, shp, jnp.float32) / np.sqrt(fan).astype(np.float32)
        return {'node_features': jax.random.normal(ks[0], (N, D), jnp.float32), 'edge_attr': jax.random.normal(ks[1], (E, EA), jnp.float32), 'edge_sh': jax.random.normal(ks[2], (E, SH), jnp.float32), 'W_node': rn(ks[3], (D, D), D), 'fc1': rn(ks[4], (EA, FC), EA), 'b1': jnp.zeros((FC,), jnp.float32), 'fc2': rn(ks[5], (FC, FC), FC), 'b2': jnp.zeros((FC,), jnp.float32), 'fc3': rn(ks[6], (FC, D), FC), 'b3': jnp.zeros((D,), jnp.float32), 'W_sh': rn(ks[7], (SH, D), SH), 'aW1': rn(ks[8], (2 * SD + EA, FC), 2 * SD + EA), 'ab1': jnp.zeros((FC,), jnp.float32), 'aW2': rn(ks[9], (FC, FC), FC), 'ab2': jnp.zeros((FC,), jnp.float32), 'aW3': rn(ks[10], (FC, H), FC), 'ab3': jnp.zeros((H,), jnp.float32), 'W_out': rn(ks[11], (D, D), D), 'edge_index': jax.random.randint(ks[12], (2, E), 0, N, jnp.int32), 'batch': jnp.zeros((N,), jnp.int32)}
    _L1_gnn_all = _L1_gnn_setup()
    _L1_gnn_in = {k: v for k, v in _L1_gnn_all.items() if k in ('W_node', 'fc1', 'b1', 'fc2', 'b2', 'fc3', 'b3', 'W_sh', 'aW1', 'ab1', 'aW2', 'ab2', 'aW3', 'ab3', 'W_out')}
    del _L1_gnn_all
    return {'x': x, 'src': src, 'dst': dst, 'edge_attr_16': edge_attr_16, 'edge_attr_32': edge_attr_32, 'L0_gnn_W_src': _L0_gnn_in['W_src'], 'L0_gnn_b_src': _L0_gnn_in['b_src'], 'L0_gnn_W_dst': _L0_gnn_in['W_dst'], 'L0_gnn_b_dst': _L0_gnn_in['b_dst'], 'L0_gnn_W_v': _L0_gnn_in['W_v'], 'L0_gnn_b_v': _L0_gnn_in['b_v'], 'L1_gnn_W_node': _L1_gnn_in['W_node'], 'L1_gnn_fc1': _L1_gnn_in['fc1'], 'L1_gnn_b1': _L1_gnn_in['b1'], 'L1_gnn_fc2': _L1_gnn_in['fc2'], 'L1_gnn_b2': _L1_gnn_in['b2'], 'L1_gnn_fc3': _L1_gnn_in['fc3'], 'L1_gnn_b3': _L1_gnn_in['b3'], 'L1_gnn_W_sh': _L1_gnn_in['W_sh'], 'L1_gnn_aW1': _L1_gnn_in['aW1'], 'L1_gnn_ab1': _L1_gnn_in['ab1'], 'L1_gnn_aW2': _L1_gnn_in['aW2'], 'L1_gnn_ab2': _L1_gnn_in['ab2'], 'L1_gnn_aW3': _L1_gnn_in['aW3'], 'L1_gnn_ab3': _L1_gnn_in['ab3'], 'L1_gnn_W_out': _L1_gnn_in['W_out']}

def reference(x, src, dst, edge_attr_16, edge_attr_32, L0_gnn_W_src, L0_gnn_b_src, L0_gnn_W_dst, L0_gnn_b_dst, L0_gnn_W_v, L0_gnn_b_v, L1_gnn_W_node, L1_gnn_fc1, L1_gnn_b1, L1_gnn_fc2, L1_gnn_b2, L1_gnn_fc3, L1_gnn_b3, L1_gnn_W_sh, L1_gnn_aW1, L1_gnn_ab1, L1_gnn_aW2, L1_gnn_ab2, L1_gnn_aW3, L1_gnn_ab3, L1_gnn_W_out):
    import jax
    import jax.numpy as jnp

    def _L0_gnn_ref(feat, W_src, b_src, W_dst, b_dst, W_v, b_v, src, dst):
        import jax, jax.numpy as jnp
        import numpy as np
        N_NODES = 6250
        N_EDGES = 100000
        IN_FEATS = 128
        HEADS = 4
        OUT_FEATS = 32
        NEG_SLOPE = 0.2

        def _edge_softmax(e, dst, n_nodes):
            seg_max = jax.ops.segment_max(e, dst, num_segments=n_nodes)
            ex = jnp.exp(e - seg_max[dst])
            seg_sum = jax.ops.segment_sum(ex, dst, num_segments=n_nodes)
            return ex / seg_sum[dst]
        n = feat.shape[0]
        f_src = (feat @ W_src.T + b_src).reshape(n, HEADS, OUT_FEATS)
        f_dst = (feat @ W_dst.T + b_dst).reshape(n, HEADS, OUT_FEATS)
        f_v = (feat @ W_v.T + b_v).reshape(n, HEADS, OUT_FEATS)
        a = f_src[src] + f_dst[dst]
        e = jnp.where(a >= 0, a, NEG_SLOPE * a)
        sa = _edge_softmax(e, dst, n)
        m = f_v[src] * sa
        rst = jax.ops.segment_sum(m, dst, num_segments=n)
        return rst.reshape(n, HEADS * OUT_FEATS)

    def _L1_gnn_ref(node_features, edge_attr, edge_sh, W_node, fc1, b1, fc2, b2, fc3, b3, W_sh, aW1, ab1, aW2, ab2, aW3, ab3, W_out, edge_index, batch):
        import jax, jax.numpy as jnp
        import numpy as np
        N, E, D, SD, SH, EA, FC, H = (6250, 100000, 128, 64, 16, 32, 128, 8)
        EPS = 1e-05
        src, dst = (edge_index[0], edge_index[1])
        x_src = node_features[src]
        h = jax.nn.silu(edge_attr @ fc1 + b1)
        h = jax.nn.silu(h @ fc2 + b2)
        scale = h @ fc3 + b3
        msg = jax.nn.silu(x_src @ W_node * scale + edge_sh @ W_sh)
        alpha_in = jnp.concatenate([x_src[:, :SD], node_features[dst, :SD], edge_attr], axis=-1)
        a = jax.nn.silu(alpha_in @ aW1 + ab1)
        a = jax.nn.silu(a @ aW2 + ab2)
        a = a @ aW3 + ab3
        alpha = jax.nn.softmax(a, axis=0)
        alpha_mean = alpha.mean(axis=1, keepdims=True)
        agg = jax.ops.segment_sum(msg * alpha_mean, dst, num_segments=node_features.shape[0])
        out = node_features + agg @ W_out
        mu = out.mean(axis=-1, keepdims=True)
        var = out.var(axis=-1, keepdims=True)
        return (out - mu) / jnp.sqrt(var + EPS)
    edge_index = jnp.stack([src, dst])
    batch0 = jnp.zeros((6250,), jnp.int32)
    h = jnp.maximum(_layernorm(x, axis=-1), 0.0)
    x = x + _L0_gnn_ref(h, L0_gnn_W_src, L0_gnn_b_src, L0_gnn_W_dst, L0_gnn_b_dst, L0_gnn_W_v, L0_gnn_b_v, src, dst)
    h = jnp.maximum(_layernorm(x, axis=-1), 0.0)
    x = x + _L1_gnn_ref(h, edge_attr_32, edge_attr_16, L1_gnn_W_node, L1_gnn_fc1, L1_gnn_b1, L1_gnn_fc2, L1_gnn_b2, L1_gnn_fc3, L1_gnn_b3, L1_gnn_W_sh, L1_gnn_aW1, L1_gnn_ab1, L1_gnn_aW2, L1_gnn_ab2, L1_gnn_aW3, L1_gnn_ab3, L1_gnn_W_out, edge_index, batch0)
    return x

_drawn_inputs = setup_inputs


def setup_inputs(seed=0):
    import zlib

    import numpy as np

    out = dict(_drawn_inputs(seed))
    spreads = {'L1_gnn_b1': (0.0, 0.8),
     'L1_gnn_b2': (0.0, 0.8),
     'L1_gnn_b3': (0.0, 0.8),
     'L1_gnn_ab1': (0.0, 0.8),
     'L1_gnn_ab2': (0.0, 0.8),
     'L1_gnn_ab3': (0.0, 0.1)}
    factors = {'edge_attr_16': 8.0,
     'edge_attr_32': 8.0,
     'L0_gnn_b_src': 8.0,
     'L0_gnn_b_dst': 8.0,
     'L0_gnn_b_v': 2.699,
     'L1_gnn_W_node': 8.0,
     'L1_gnn_fc1': 8.0,
     'L1_gnn_fc2': 8.0,
     'L1_gnn_fc3': 8.0,
     'L1_gnn_W_sh': 8.0,
     'L1_gnn_aW1': 8.0,
     'L1_gnn_aW2': 8.0,
     'L1_gnn_aW3': 8.0,
     'L1_gnn_W_out': 8.0}
    for name, (base, spread) in spreads.items():
        noise = np.random.default_rng([zlib.crc32(name.encode()), seed]).standard_normal(out[name].shape)
        drawn = base * np.exp(spread * noise) if base else spread * noise
        out[name] = jnp.asarray(drawn.astype(out[name].dtype))
    for name, factor in factors.items():
        out[name] = (out[name] * factor).astype(out[name].dtype)
    return out
```

```python
from contextlib import ExitStack

import concourse.bass as bass
from concourse import mybir

F32 = mybir.dt.float32
BF16 = mybir.dt.bfloat16
I32 = mybir.dt.int32
ALU = mybir.AluOpType
ACT = mybir.ActivationFunctionType
AX_X = mybir.AxisListType.X
RMAX = bass.bass_isa.ReduceOp.max
RADD = bass.bass_isa.ReduceOp.add

P = 128
N = 6250
E = 106250
C = 128
NB = -(-N // P)
NBT = NB + 1
NP = NBT * P
IT = 512
TJ = IT // P
NI = (E + NB * (IT - 1)) // IT
OFF_MAX = -(-E // IT) * IT
EQ = -(-(OFF_MAX + IT) // P)
EP = EQ * P
HEADS = 8
EA = 32
SH = 16
SLOPE = 0.2
EPS = 1e-5
FAR = -3.0e38
NO_NODE = 8191
OFF_RANGE = 16384.0
U = 4
LAPS = NI // U
assert NI % U == 0 and NBT % 2 == 0 and (OFF_MAX + IT) <= EP


def item(lap, u, d=0, turn=U):
    v = u + d
    return (lap + v // turn) * turn + v % turn, v % turn, lap + v // turn


def after(i, n):
    return not isinstance(i, int) or i >= n


def exists(i, count):
    return not isinstance(i, int) or 0 <= i < count


def hold(eng, passed, *waits):
    for sem, n in waits:
        eng.wait_ge(sem, n)
        eng.sem_inc(passed, 1)


def run_items(eng, step, turns=LAPS, turn=U):
    for lap in (-1, 0):
        for u in range(turn):
            step(lap, u)
    with eng.Fori(1, turns - 1) as lap:
        for u in range(turn):
            step(lap, u)
    for lap in (turns - 1, turns):
        for u in range(turn):
            step(lap, u)


def build(nc, x, src_pad, dst_pad, ea32, ea16, w0cat, b0cat, w1cat, fc1, b1, fc2, b2, fc3, b3, w_sh,
          aw1e, ab1, aw2, ab2, aw3, ab3, w_out, out):
    top = ExitStack()
    with top:
        def sb(name, shape, dt, stack=top):
            return stack.enter_context(nc.sbuf_tensor(name, shape, dt))

        def ps(name, shape, dt=F32, stack=top):
            return stack.enter_context(nc.psum_tensor(name, shape, dt))

        def sem(name, stack=top):
            return stack.enter_context(nc.semaphore(name))

        sp_passed = sem("sp_passed")
        pool_passed = sem("pool_passed")

        def dram(name, shape, dt):
            return nc.dram_tensor(name, shape, dt).ap()

        pen_d = dram("pen_d", [EP], BF16)
        low_d = dram("low_d", [EP], BF16)
        pair_d = dram("pair_d", [EP, 2], F32)
        items_d = dram("items_d", [NI, 4], I32)
        base_d = dram("base_d", [NI], F32)
        rows_d = [dram(f"rows{l}_d", [NP, 2 * C], F32) for l in range(2)]
        dst_d = [dram(f"dst{l}_d", [NP, 3 * C], BF16) for l in range(2)]
        msg_d = dram("msg_d", [NI, P, TJ * C], F32)

        ident = sb("ident", [P, P], F32)
        iota_row = sb("iota_row", [P, P], F32)
        iota_col = sb("iota_col", [P, 2], F32)
        items_row = sb("items_row", [1, NI * 4], I32)
        base_bc = sb("base_bc", [P, NI], F32)
        local = sb("local", [P, NI * TJ], F32)
        X = sb("X", [P, NBT, C], F32)
        H = sb("H", [P, NBT, C], F32)
        big = sb("big", [P, NBT * 2 * C + NI * TJ * HEADS // 4], F32)
        acc0 = big[:, 0:NBT * 2 * C]
        acc1 = big[:, 0:NBT * C]
        logits = big[:, NBT * C:NBT * C + NI * TJ * HEADS]
        scratch = big[:, 0:NBT * C].rearrange("p (n c) -> p n c", c=C)
        assert NBT * C + NI * TJ * HEADS <= big.shape[1]

        x_v = x.rearrange("(n p) c -> p n c", p=P)


        def norm_vector(eng, chain, source, to_act, from_act, stats, target, relu):
            def link(ins):
                chain[1] += 1
                ins.then_inc(chain[0], 1)
                eng.wait_ge(chain[0], chain[1])
            mean, var, rstd = (stats[:, k, :] for k in range(3))

            def wide(v):
                return v.unsqueeze(2).to_broadcast([P, NBT, C])
            link(nc.vector.tensor_reduce(mean, source, AX_X, ALU.add))
            link(nc.vector.tensor_scalar(mean, mean, 1.0 / C, None, ALU.mult))
            link(nc.vector.tensor_tensor(target, source, wide(mean), ALU.subtract))
            link(nc.vector.tensor_tensor(scratch, target, target, ALU.mult))
            link(nc.vector.tensor_reduce(var, scratch, AX_X, ALU.add))
            nc.vector.tensor_scalar(var, var, 1.0 / C, EPS, ALU.mult, ALU.add).then_inc(to_act, 1)
            eng.wait_ge(from_act, 1)
            link(nc.vector.reciprocal(rstd, rstd))
            if relu:
                link(nc.vector.scalar_tensor_tensor(out=target, in0=target, scalar=0.0, in1=wide(rstd),
                                                    op0=ALU.max, op1=ALU.mult))
            else:
                link(nc.vector.tensor_tensor(target, target, wide(rstd), ALU.mult))

        def norm_scalar(eng, stats, to_act, from_act):
            eng.wait_ge(to_act, 1)
            nc.scalar.activation(stats[:, 2, :], stats[:, 1, :], ACT.Sqrt).then_inc(from_act, 1)

        def index_pass():
            st = ExitStack()
            with st:
                before = sb("before", [P, EQ], I32, st)
                here = sb("here", [P, EQ], I32, st)
                behind = sb("behind", [P, EQ], I32, st)
                here_f = sb("here_f", [P, EQ], F32, st)
                flag = sb("flag", [P, EQ], F32, st)
                pen = sb("pen", [P, EQ], BF16, st)
                low_i = sb("low_i", [P, EQ], I32, st)
                low = sb("low", [P, EQ], BF16, st)
                pair = sb("pair", [P, EQ, 2], F32, st)
                junk = sb("junk", [P, EQ], BF16, st)
                count = sb("count", [P, NBT], F32, st)
                ones = sb("ones", [P, P], F32, st)
                first = sb("first", [P, NBT], F32, st)
                row = sb("row", [P, 8, NB], F32, st)
                tiles_i = sb("tiles_i", [P, NB], I32, st)
                pick = sb("pick", [P, 8], F32, st)
                table = sb("table", [P, 2, 4], I32, st)
                base = sb("base", [P, 2], F32, st)
                total = ps("total", [P, NBT], F32, st)
                s_in = sem("ip_in", st)
                s_const = sem("ip_const", st)
                s_chain = sem("ip_chain", st)
                s_rows = sem("ip_rows", st)
                s_count = sem("ip_count", st)
                s_total = sem("ip_total", st)
                s_table = sem("ip_table", st)
                s_out = sem("ip_out", st)
                s_items = sem("ip_items", st)
                s_back = sem("ip_back", st)
                with nc.Block() as block:
                    @block.sync
                    def _(sp):
                        for k, t in enumerate((before, here, behind)):
                            sp.dma_start(t[:, :], dst_pad[k:k + EP].rearrange("(p q) -> p q", q=EQ)).then_inc(s_in, 16)
                        sp.wait_ge(s_rows, 3)
                        sp.dma_start(pen_d.rearrange("(p q) -> p q", q=EQ), pen[:, :]).then_inc(s_out, 16)
                        sp.dma_start(low_d.rearrange("(p q) -> p q", q=EQ), low[:, :]).then_inc(s_out, 16)
                        sp.dma_start(pair_d.rearrange("(p q) k -> p q k", q=EQ), pair[:, :, :]).then_inc(s_out, 16)
                        sp.wait_ge(s_table, 2)
                        for g in range(2):
                            sp.dma_start(items_d[g * P:(g + 1) * P, :], table[:, g, :]).then_inc(s_items, 16)
                            sp.dma_start(base_d[g * P:(g + 1) * P].rearrange("(p k) -> p k", k=1),
                                         base[:, g:g + 1]).then_inc(s_items, 16)
                        sp.wait_ge(s_items, 64)
                        sp.dma_start(items_row[:, :], items_d.rearrange("(a i) k -> a (i k)", a=1)).then_inc(s_back, 16)
                        sp.dma_start(base_bc[:, :], base_d.partition_broadcast(P)).then_inc(s_back, 16)
                        sp.wait_ge(s_back, 32)
                        sp.wait_ge(s_out, 48)

                    @block.gpsimd
                    def _(pool):
                        nc.gpsimd.memset(ident[:, :], 0.0).then_inc(s_const, 1)
                        pool.wait_ge(s_const, 1)
                        nc.gpsimd.affine_select(out=ident[:, :], in_=ident[:, :], compare_op=ALU.not_equal, fill=1.0,
                                                base=0, pattern=[[-1, P]], channel_multiplier=1).then_inc(s_const, 1)
                        nc.gpsimd.iota(iota_row[:, :], [[1, P]], base=0, channel_multiplier=0,
                                       allow_small_or_imprecise_dtypes=True).then_inc(s_const, 1)
                        nc.gpsimd.iota(iota_col[:, :], [[P, 2]], base=0, channel_multiplier=1,
                                       allow_small_or_imprecise_dtypes=True).then_inc(s_const, 1)
                        nc.gpsimd.memset(ones[:, :], 1.0).then_inc(s_const, 1)
                        nc.gpsimd.memset(table[:, :, :], 0).then_inc(s_const, 1)

                    @block.tensor
                    def _(pe):
                        pe.wait_ge(s_const, 6)
                        pe.wait_ge(s_count, NBT)
                        nc.tensor.matmul(total[:, :], ones[:, :], count[:, :], start=True, stop=True).then_inc(s_total, 1)

                    @block.vector
                    def _(dve):
                        chain = [0]

                        def link(ins):
                            chain[0] += 1
                            ins.then_inc(s_chain, 1)
                            dve.wait_ge(s_chain, chain[0])
                        dve.wait_ge(s_in, 48)
                        link(nc.vector.tensor_tensor(flag[:, :], here[:, :], before[:, :], ALU.not_equal))
                        nc.vector.tensor_scalar(pen[:, :], flag[:, :], FAR, None, ALU.mult).then_inc(s_rows, 1)
                        link(nc.vector.tensor_scalar(low_i[:, :], here[:, :], P - 1, None, ALU.bitwise_and))
                        nc.vector.tensor_copy(low[:, :], low_i[:, :]).then_inc(s_rows, 1)
                        link(nc.vector.tensor_copy(here_f[:, :], here[:, :]))
                        nc.vector.tensor_copy(pair[:, :, 0], here_f[:, :])
                        link(nc.vector.tensor_tensor(flag[:, :], here[:, :], behind[:, :], ALU.is_equal))
                        nc.vector.scalar_tensor_tensor(out=pair[:, :, 1], in0=flag[:, :], scalar=OFF_RANGE,
                                                       in1=here_f[:, :], op0=ALU.mult, op1=ALU.add).then_inc(s_rows, 1)
                        for b in range(NBT):
                            if b:
                                dve.wait_ge(s_count, b)
                            nc.vector.tensor_scalar(junk[:, :], here_f[:, :], float(P * b), 0.0, ALU.is_lt,
                                                    ALU.add, accum_out=count[:, b:b + 1]).then_inc(s_count, 1)
                        dve.wait_ge(s_total, 1)
                        link(nc.vector.tensor_copy(first[:, :], total[:, :]))
                        n_up, tiles, incl, excl, q0, ge, gx, zero = (row[:, k, :] for k in range(8))
                        link(nc.vector.tensor_tensor(n_up, first[:, 1:NBT], first[:, 0:NB], ALU.subtract))
                        link(nc.vector.tensor_scalar(tiles_i[:, :], n_up, float(IT - 1), None, ALU.add))
                        link(nc.vector.tensor_scalar(tiles_i[:, :], tiles_i[:, :], IT.bit_length() - 1, None,
                                                     ALU.arith_shift_right))
                        link(nc.vector.tensor_copy(tiles, tiles_i[:, :]))
                        link(nc.vector.memset(zero, 0.0))
                        link(nc.vector.tensor_tensor_scan(incl, zero, tiles, 0.0, ALU.add, ALU.add))
                        link(nc.vector.tensor_tensor(excl, incl, tiles, ALU.subtract))
                        link(nc.vector.scalar_tensor_tensor(out=q0, in0=excl, scalar=-float(IT), in1=first[:, 0:NB],
                                                            op0=ALU.mult, op1=ALU.add))
                        dve.wait_ge(s_const, 6)
                        for g in range(2):
                            me = iota_col[:, g:g + 1]
                            nb, off = pick[:, 4 * g:4 * g + 1], pick[:, 4 * g + 1:4 * g + 2]
                            link(nc.vector.tensor_scalar(ge, incl, me, None, ALU.is_le))
                            link(nc.vector.tensor_scalar(gx, excl, me, None, ALU.is_le))
                            link(nc.vector.tensor_reduce(nb, ge, AX_X, ALU.add))
                            link(nc.vector.tensor_tensor(gx, gx, ge, ALU.subtract))
                            link(nc.vector.tensor_tensor(gx, gx, q0, ALU.mult))
                            link(nc.vector.tensor_reduce(off, gx, AX_X, ALU.add))
                            link(nc.vector.scalar_tensor_tensor(out=off, in0=me, scalar=float(IT), in1=off,
                                                                op0=ALU.mult, op1=ALU.add))
                            link(nc.vector.tensor_scalar(table[:, g, 0:1], off, float(OFF_MAX), None, ALU.min))
                            link(nc.vector.tensor_scalar(table[:, g, 1:2], nb, float(P), None, ALU.mult))
                            link(nc.vector.tensor_scalar(table[:, g, 2:3], nb, float(2 * C), None, ALU.mult))
                            nc.vector.tensor_scalar(base[:, g:g + 1], nb, float(P), None, ALU.mult).then_inc(s_table, 1)

        def node_tables(layer, w_dram, bias_dram):
            st = ExitStack()
            with st:
                pre = f"n{layer}_"
                wcat = sb(pre + "wcat", [P, 3 * C], F32, st)
                bias = sb(pre + "bias", [P, 3 * C], F32, st)
                stats = sb(pre + "stats", [P, 3, NBT], F32, st)
                h_b = sb(pre + "h_b", [P, 2, C], F32, st)
                h_t = sb(pre + "h_t", [P, 2, C], F32, st)
                row = sb(pre + "row", [P, 2, 3 * C], F32, st)
                rest = sb(pre + "rest", [P, 2, C], F32, st)
                split = sb(pre + "split", [P, 2, 3 * C], BF16, st)
                tp = [ps(pre + f"tp{k}", [P, C], F32, st) for k in range(2)]
                pp = [ps(pre + f"pp{k}", [P, 3 * C], F32, st) for k in range(2)]
                s_in = sem(pre + "in", st)
                s_x = sem(pre + "x", st)
                s_chain = sem(pre + "chain", st)
                s_var = sem(pre + "var", st)
                s_root = sem(pre + "root", st)
                s_h = sem(pre + "h", st)
                s_hb = sem(pre + "hb_ready", st)
                s_tp = sem(pre + "tp_ready", st)
                s_ht = sem(pre + "ht_ready", st)
                s_pp = sem(pre + "pp_ready", st)
                s_row = sem(pre + "row_ready", st)
                s_split = sem(pre + "split_ready", st)
                s_step = sem(pre + "split_step", st)
                s_store = [sem(pre + f"store{k}", st) for k in range(2)]
                with nc.Block() as block:
                    @block.sync
                    def _(sp):
                        if layer == 0:
                            for k in range(2):
                                a, b = k * NBT // 2, (k + 1) * NBT // 2
                                sp.dma_start(X[:, a:b, :], x_v[:, a:b, :]).then_inc(s_x, 16)
                        sp.dma_start(wcat[:, :], w_dram).then_inc(s_in, 16)
                        if bias_dram is not None:
                            sp.dma_start(bias[:, :], bias_dram.partition_broadcast(P)).then_inc(s_in, 16)

                        def step(lap, u):
                            i, s, _ = item(lap, u, 0, 2)
                            if not exists(i, NBT):
                                return
                            sp.wait_ge(s_row, i + 1)
                            sp.dma_start(rows_d[layer][bass.ds(i * P, P), :], row[:, s, 0:2 * C]).then_inc(s_store[s], 16)
                            sp.wait_ge(s_split, i + 1)
                            sp.dma_start(dst_d[layer][bass.ds(i * P, P), :], split[:, s, :]).then_inc(s_store[s], 16)
                        run_items(sp, step, NBT // 2, 2)
                        for k in range(2):
                            sp.wait_ge(s_store[k], 32 * (NBT // 2))

                    @block.tensor
                    def _(pe):
                        pe.wait_ge(s_in, 16 if bias_dram is None else 32)

                        def step(lap, u):
                            i, s, _ = item(lap, u, 1, 2)
                            if exists(i, NBT):
                                if after(i, 2):
                                    pe.wait_ge(s_ht, i - 1)
                                pe.wait_ge(s_hb, i + 1)
                                nc.tensor.transpose(tp[s][:, :], h_b[:, s, :], ident[:, :]).then_inc(s_tp, 1)
                            i, s, _ = item(lap, u, 0, 2)
                            if exists(i, NBT):
                                pe.wait_ge(s_ht, i + 1)
                                if after(i, 2):
                                    pe.wait_ge(s_row, i - 1)
                                nc.tensor.matmul(pp[s][:, :], h_t[:, s, :], wcat[:, :], start=True,
                                                 stop=True).then_inc(s_pp, 1)
                        run_items(pe, step, NBT // 2, 2)

                    @block.gpsimd
                    def _(pool):
                        pool.wait_ge(s_h, 1)

                        def step(lap, u):
                            i, s, _ = item(lap, u, 0, 2)
                            if not exists(i, NBT):
                                return
                            if after(i, 2):
                                pool.wait_ge(s_tp, i - 1)
                            nc.gpsimd.tensor_copy(h_b[:, s, :], H[:, bass.ds(i, 1), :].rearrange("p n c -> p (n c)")).then_inc(s_hb, 1)
                        run_items(pool, step, NBT // 2, 2)

                    @block.scalar
                    def _(act):
                        norm_scalar(act, stats, s_var, s_root)

                        def step(lap, u):
                            i, s, _ = item(lap, u, 0, 2)
                            if not exists(i, NBT):
                                return
                            act.wait_ge(s_tp, i + 1)
                            if after(i, 2):
                                act.wait_ge(s_pp, i - 1)
                            nc.scalar.activation(h_t[:, s, :], tp[s][:, :], ACT.Copy).then_inc(s_ht, 1)
                        run_items(act, step, NBT // 2, 2)

                    @block.vector
                    def _(dve):
                        chain = [s_chain, 0]
                        if layer == 0:
                            dve.wait_ge(s_x, 32)
                        else:
                            for n in range(NBT):
                                w = acc0[:, n * 2 * C:n * 2 * C + C]
                                v = acc0[:, n * 2 * C + C:(n + 1) * 2 * C]
                                nc.vector.tensor_scalar(w, w, 0.5, None, ALU.max).then_inc(s_chain, 1)
                            dve.wait_ge(s_chain, NBT)
                            for n in range(NBT):
                                w = acc0[:, n * 2 * C:n * 2 * C + C]
                                nc.vector.reciprocal(w, w).then_inc(s_chain, 1)
                            dve.wait_ge(s_chain, 2 * NBT)
                            for n in range(NBT):
                                w = acc0[:, n * 2 * C:n * 2 * C + C]
                                v = acc0[:, n * 2 * C + C:(n + 1) * 2 * C]
                                nc.vector.tensor_tensor(w, w, v, ALU.mult).then_inc(s_chain, 1)
                            dve.wait_ge(s_chain, 3 * NBT)
                            for n in range(NBT):
                                w = acc0[:, n * 2 * C:n * 2 * C + C]
                                nc.vector.tensor_tensor(X[:, n, :], X[:, n, :], w, ALU.add).then_inc(s_chain, 1)
                            dve.wait_ge(s_chain, 4 * NBT)
                            chain[1] = 4 * NBT
                        norm_vector(dve, chain, X[:, :, :], s_var, s_root, stats, H[:, :, :], True)
                        nc.vector.tensor_copy(stats[:, 0, 0:1], stats[:, 0, 0:1]).then_inc(s_h, 1)
                        if bias_dram is not None:
                            dve.wait_ge(s_in, 32)

                        def step(lap, u):
                            i, s, _ = item(lap, u, 0, 2)
                            if not exists(i, NBT):
                                return
                            dve.wait_ge(s_pp, i + 1)
                            if after(i, 2):
                                dve.wait_ge(s_store[s], 32 * item(lap, u, 0, 2)[2])
                            if bias_dram is None:
                                nc.vector.tensor_copy(row[:, s, :], pp[s][:, :]).then_inc(s_row, 1)
                            else:
                                nc.vector.tensor_tensor(row[:, s, :], pp[s][:, :], bias[:, :], ALU.add).then_inc(s_row, 1)
                            dve.wait_ge(s_row, i + 1)
                            part = row[:, s, 2 * C:3 * C]
                            hi, mid, lo = (split[:, s, k * C:(k + 1) * C] for k in range(3))
                            nc.vector.tensor_copy(hi, part).then_inc(s_step, 1)
                            dve.wait_ge(s_step, i * 3 + 1)
                            nc.vector.tensor_tensor(rest[:, s, :], part, hi, ALU.subtract).then_inc(s_step, 1)
                            dve.wait_ge(s_step, i * 3 + 2)
                            nc.vector.tensor_copy(mid, rest[:, s, :]).then_inc(s_step, 1)
                            dve.wait_ge(s_step, i * 3 + 3)
                            nc.vector.tensor_tensor(lo, rest[:, s, :], mid, ALU.subtract).then_inc(s_split, 1)
                        run_items(dve, step, NBT // 2, 2)

        def layer0_edges():
            st = ExitStack()
            with st:
                sidx = [sb(f"l0_sidx{k}", [P, TJ], I32, st) for k in range(U)]
                G = sb("l0_G", [P, U, TJ, 2 * C], F32, st)
                lo_t = sb("l0_lo", [P, U, IT], BF16, st)
                pen_t = sb("l0_pen", [P, U, IT], BF16, st)
                fd_t = sb("l0_fd", [P, U, 3 * C], BF16, st)
                pair_t = sb("l0_pair", [P, U, TJ, 2], F32, st)
                ends_t = sb("l0_ends", [P, U, TJ], F32, st)
                oht = sb("l0_oht", [P, U, IT], BF16, st)
                e_t = sb("l0_e", [P, U, IT], F32, st)
                m_t = sb("l0_m", [P, 2, IT + 1], F32, st)
                d_t = sb("l0_d", [P, 2, IT], F32, st)
                wv_t = sb("l0_wv", [P, 2, IT], F32, st)
                s_t = sb("l0_s", [P, 2, IT], F32, st)
                r_t = sb("l0_r", [P, 2, IT], F32, st)
                ends = sb("l0_sel", [P, 2, TJ, P], F32, st)
                sr_e = sb("l0_sre", [P, 2, TJ, 2 * C], F32, st)
                A = [ps(f"l0_A{k}", [P, IT], F32, st) for k in range(2)]
                V = [ps(f"l0_V{k}", [P, IT], F32, st) for k in range(2)]
                sr_p = [ps(f"l0_srp{k}", [P, 2, 2 * C], F32, st) for k in range(2)]
                accp = ps("l0_accp", [P, 2 * C], F32, st)
                ld = [sem(f"l0_ld{k}", st) for k in range(U)]
                gat = [sem(f"l0_gat{k}", st) for k in range(U)]
                oht_ready = sem("l0_oht_ready", st)
                pairs_done = sem("l0_pairs_done", st)
                a_ready = sem("l0_a_ready", st)
                v_ready = sem("l0_v_ready", st)
                a_copied = sem("l0_a_copied", st)
                e_ready = sem("l0_e_ready", st)
                carry_ready = sem("l0_carry_ready", st)
                m_ready = sem("l0_m_ready", st)
                z_ready = sem("l0_z_ready", st)
                gap_ready = sem("l0_gap_ready", st)
                d_ready = sem("l0_d_ready", st)
                w_ready = sem("l0_w_ready", st)
                c_ready = sem("l0_c_ready", st)
                wv_ready = sem("l0_wv_ready", st)
                s_ready = sem("l0_s_ready", st)
                r_ready = sem("l0_r_ready", st)
                srt_ready = sem("l0_srt_ready", st)
                sre_ready = sem("l0_sre_ready", st)
                sel_ready = sem("l0_sel_ready", st)
                accp_ready = sem("l0_accp_ready", st)
                acc_done = sem("l0_acc_done", st)
                zeroed = sem("l0_zeroed", st)
                with nc.Block() as block:
                    @block.sync
                    def _(sp):
                        def step(lap, u):
                            i, s, lp = item(lap, u)
                            if not exists(i, NI):
                                return
                            off = sp.value_load(items_row[0:1, bass.ds(i * 4, 1)], min_val=0, max_val=OFF_MAX)
                            row = sp.value_load(items_row[0:1, bass.ds(i * 4 + 1, 1)], min_val=0, max_val=NB * P)
                            if after(i, U):
                                hold(sp, sp_passed,
                                     (gat[s], 16 * TJ * lp),
                                     (a_ready, i - U + 1),
                                     (d_ready, i - U + 1),
                                     (pairs_done, 2 * (i - U + 1)))
                            sp.dma_start(sidx[s][:, :], src_pad[bass.ds(off, IT)].rearrange("(p j) -> p j", j=TJ)).then_inc(ld[s], 16)
                            sp.dma_start(lo_t[:, s, :], low_d[bass.ds(off, IT)].partition_broadcast(P)).then_inc(ld[s], 16)
                            sp.dma_start(pen_t[:, s, :], pen_d[bass.ds(off, IT)].partition_broadcast(P)).then_inc(ld[s], 16)
                            sp.dma_start(fd_t[:, s, :], dst_d[0][bass.ds(row, P), :]).then_inc(ld[s], 16)
                            sp.dma_start(pair_t[:, s, :, :], pair_d[bass.ds(off, IT), :].rearrange("(p j) k -> p j k", j=TJ)).then_inc(ld[s], 16)
                        run_items(sp, step)

                    @block.gpsimd
                    def _(pool):
                        def gap(lap, u, d):
                            i, s, _ = item(lap, u, d)
                            if not exists(i, NI):
                                return
                            b = s % 2
                            hold(pool, pool_passed, (m_ready, i + 1))
                            if after(i, 2):
                                hold(pool, pool_passed, (s_ready, i - 1), (r_ready, i - 1))
                            nc.gpsimd.tensor_tensor(d_t[:, b, :], m_t[:, b, 0:IT], m_t[:, b, 1:IT + 1],
                                                    ALU.subtract).then_inc(gap_ready, 1)
                            pool.wait_ge(gap_ready, i + 1)
                            nc.gpsimd.tensor_tensor(d_t[:, b, :], d_t[:, b, :], pen_t[:, s, :], ALU.add).then_inc(d_ready, 1)

                        def select(lap, u, d):
                            i, s, _ = item(lap, u, d)
                            if not exists(i, NI):
                                return
                            b = s % 2
                            hold(pool, pool_passed, (pairs_done, 2 * (i + 1)))
                            if after(i, 2):
                                hold(pool, pool_passed, (accp_ready, i - 1))
                            for j in range(TJ):
                                nc.gpsimd.tensor_scalar(ends[:, b, j, :], iota_row[:, :], ends_t[:, s, j:j + 1], None,
                                                        ALU.is_equal).then_inc(sel_ready, 1)

                        def gather(lap, u, d):
                            i, s, lp = item(lap, u, d)
                            if not exists(i, NI):
                                return
                            if after(i, U):
                                hold(pool, pool_passed, (v_ready, i - U + 1))
                            hold(pool, pool_passed, (ld[s], 80 * (lp + 1)))
                            for j in range(TJ):
                                nc.gpsimd.indirect_dma_start(
                                    out=G[:, s, j, :], out_offset=None, in_=rows_d[0][:, :],
                                    in_offset=bass.IndirectOffsetOnAxis(ap=sidx[s][:, j:j + 1], axis=0)).then_inc(gat[s], 16)

                        def step(lap, u):
                            gather(lap, u, 3)
                            gap(lap, u, 1)
                            select(lap, u, 0)
                        run_items(pool, step)

                    @block.tensor
                    def _(pe):
                        def front(lap, u, d):
                            i, s, lp = item(lap, u, d)
                            if not exists(i, NI):
                                return
                            b = s % 2
                            pe.wait_ge(gat[s], 16 * TJ * (lp + 1))
                            pe.wait_ge(ld[s], 80 * (lp + 1))
                            pe.wait_ge(oht_ready, i + 1)
                            if after(i, 2):
                                pe.wait_ge(a_copied, i - 1)
                            av = A[b][:, :].rearrange("p (e j) -> p j e", j=TJ)
                            vv = V[b][:, :].rearrange("p (e j) -> p j e", j=TJ)
                            for j in range(TJ):
                                nc.tensor.matmul(av[:, j, :], G[:, s, j, 0:C], ident[:, :], is_transpose=True,
                                                 start=(j == 0), stop=False, skip_group_check=True)
                            for k in range(3):
                                last = nc.tensor.matmul(A[b][:, :], fd_t[:, s, k * C:(k + 1) * C], oht[:, s, :],
                                                        start=False, stop=(k == 2), skip_group_check=True)
                            last.then_inc(a_ready, 1)
                            if after(i, 2):
                                pe.wait_ge(wv_ready, i - 1)
                            for j in range(TJ):
                                last = nc.tensor.matmul(vv[:, j, :], G[:, s, j, C:2 * C], ident[:, :], is_transpose=True,
                                                        start=(j == 0), stop=(j == TJ - 1), skip_group_check=True)
                            last.then_inc(v_ready, 1)

                        def turn(lap, u, d):
                            i, s, _ = item(lap, u, d)
                            if not exists(i, NI):
                                return
                            b = s % 2
                            pe.wait_ge(s_ready, i + 1)
                            pe.wait_ge(r_ready, i + 1)
                            if after(i, 1):
                                pe.wait_ge(sre_ready, 2 * i)
                            for j in range(TJ):
                                for k, t in enumerate((s_t, r_t)):
                                    tv = t[:, b, :].rearrange("p (e j) -> p j e", j=TJ)
                                    last = nc.tensor.matmul(sr_p[j // 2][:, j % 2, k * C:(k + 1) * C], tv[:, j, :],
                                                            ident[:, :], is_transpose=True,
                                                            start=(j % 2 == 0 and k == 0), stop=(j % 2 == 1 and k == 1),
                                                            skip_group_check=True)
                                if j % 2:
                                    last.then_inc(srt_ready, 1)

                        def collect(lap, u, d):
                            i, s, _ = item(lap, u, d)
                            if not exists(i, NI):
                                return
                            b = s % 2
                            pe.wait_ge(sel_ready, TJ * (i + 1))
                            pe.wait_ge(sre_ready, 2 * (i + 1))
                            if after(i, 1):
                                pe.wait_ge(acc_done, i)
                            for j in range(TJ):
                                last = nc.tensor.matmul(accp[:, :], ends[:, b, j, :], sr_e[:, b, j, :],
                                                        start=(j == 0), stop=(j == TJ - 1))
                            last.then_inc(accp_ready, 1)

                        def step(lap, u):
                            front(lap, u, 2)
                            collect(lap, u, -1)
                            turn(lap, u, 0)
                        run_items(pe, step)

                    @block.scalar
                    def _(act):
                        def bring(lap, u, d):
                            i, s, _ = item(lap, u, d)
                            if not exists(i, NI):
                                return
                            act.wait_ge(a_ready, i + 1)
                            if after(i, U):
                                act.wait_ge(s_ready, i - U + 1)
                                act.wait_ge(wv_ready, i - U + 1)
                            nc.scalar.activation(e_t[:, s, :], A[s % 2][:, :], ACT.Copy).then_inc(a_copied, 1)

                        def exps(lap, u, d):
                            i, s, _ = item(lap, u, d)
                            if not exists(i, NI):
                                return
                            act.wait_ge(z_ready, i + 1)
                            nc.scalar.activation(e_t[:, s, :], e_t[:, s, :], ACT.Exp).then_inc(w_ready, 1)
                            act.wait_ge(d_ready, i + 1)
                            nc.scalar.activation(d_t[:, s % 2, :], d_t[:, s % 2, :], ACT.Exp).then_inc(c_ready, 1)

                        def evacuate(lap, u, d):
                            i, s, _ = item(lap, u, d)
                            if not exists(i, NI):
                                return
                            b = s % 2
                            if after(i, 2):
                                act.wait_ge(accp_ready, i - 1)
                            for k in range(2):
                                act.wait_ge(srt_ready, 2 * i + k + 1)
                                nc.scalar.activation(sr_e[:, b, 2 * k:2 * k + 2, :], sr_p[k][:, :, :],
                                                     ACT.Copy).then_inc(sre_ready, 1)

                        def step(lap, u):
                            bring(lap, u, 2)
                            exps(lap, u, 1)
                            evacuate(lap, u, -1)
                        run_items(act, step)

                    @block.vector
                    def _(dve):
                        nc.vector.memset(acc0, 0.0).then_inc(zeroed, 1)
                        nc.vector.memset(m_t[:, :, :], 0.0).then_inc(zeroed, 1)
                        nc.vector.memset(s_t[:, :, :], 0.0).then_inc(zeroed, 1)
                        nc.vector.memset(r_t[:, :, :], 0.0).then_inc(zeroed, 1)
                        dve.wait_ge(zeroed, 4)

                        def onehot(lap, u, d):
                            i, s, lp = item(lap, u, d)
                            if not exists(i, NI):
                                return
                            dve.wait_ge(ld[s], 80 * (lp + 1))
                            if after(i, U):
                                dve.wait_ge(sel_ready, TJ * (i - U + 1))
                            nc.vector.tensor_scalar(oht[:, s, :], lo_t[:, s, :], iota_col[:, 0:1], None,
                                                    ALU.is_equal).then_inc(oht_ready, 1)
                            mine = base_bc[:, bass.ds(i, 1)].to_broadcast([P, TJ])
                            nc.vector.tensor_tensor(local[:, bass.ds(i * TJ, TJ)], pair_t[:, s, :, 0], mine,
                                                    ALU.subtract).then_inc(pairs_done, 1)
                            nc.vector.tensor_tensor(ends_t[:, s, :], pair_t[:, s, :, 1], mine,
                                                    ALU.subtract).then_inc(pairs_done, 1)

                        def maximum(lap, u, d):
                            i, s, lp = item(lap, u, d)
                            if not exists(i, NI):
                                return
                            b = s % 2
                            dve.wait_ge(ld[s], 80 * (lp + 1))
                            dve.wait_ge(a_copied, i + 1)
                            nc.vector.scalar_tensor_tensor(out=e_t[:, s, :], in0=e_t[:, s, :], scalar=SLOPE, in1=e_t[:, s, :],
                                                           op0=ALU.mult, op1=ALU.max).then_inc(e_ready, 1)
                            dve.wait_ge(e_ready, i + 1)
                            if after(i, 2):
                                dve.wait_ge(d_ready, i - 1)
                            nc.vector.tensor_copy(m_t[:, b, 0:1], m_t[:, 1 - b, IT:IT + 1]).then_inc(carry_ready, 1)
                            dve.wait_ge(carry_ready, i + 1)
                            nc.vector.tensor_tensor_scan(m_t[:, b, 1:IT + 1], pen_t[:, s, :], e_t[:, s, :],
                                                         m_t[:, b, 0:1], ALU.add, ALU.max).then_inc(m_ready, 1)
                            dve.wait_ge(m_ready, i + 1)
                            nc.vector.tensor_tensor(e_t[:, s, :], e_t[:, s, :], m_t[:, b, 1:IT + 1],
                                                    ALU.subtract).then_inc(z_ready, 1)

                        def sums(lap, u, d):
                            i, s, _ = item(lap, u, d)
                            if not exists(i, NI):
                                return
                            b = s % 2
                            dve.wait_ge(w_ready, i + 1)
                            dve.wait_ge(v_ready, i + 1)
                            nc.vector.tensor_tensor(wv_t[:, b, :], e_t[:, s, :], V[b][:, :], ALU.mult).then_inc(wv_ready, 1)
                            dve.wait_ge(c_ready, i + 1)
                            if after(i, 2):
                                dve.wait_ge(srt_ready, 2 * (i - 1))
                            if after(i, 1):
                                dve.wait_ge(s_ready, i)
                                dve.wait_ge(r_ready, i)
                            nc.vector.tensor_tensor_scan(s_t[:, b, :], d_t[:, b, :], e_t[:, s, :],
                                                         s_t[:, 1 - b, IT - 1:IT], ALU.mult, ALU.add).then_inc(s_ready, 1)
                            dve.wait_ge(wv_ready, i + 1)
                            nc.vector.tensor_tensor_scan(r_t[:, b, :], d_t[:, b, :], wv_t[:, b, :],
                                                         r_t[:, 1 - b, IT - 1:IT], ALU.mult, ALU.add).then_inc(r_ready, 1)

                        def add(lap, u, d):
                            i, s, _ = item(lap, u, d)
                            if not exists(i, NI):
                                return
                            at = dve.value_load(items_row[0:1, bass.ds(i * 4 + 2, 1)], min_val=0, max_val=NB * 2 * C)
                            dve.wait_ge(accp_ready, i + 1)
                            if after(i, 1):
                                dve.wait_ge(acc_done, i)
                            mine = acc0[:, bass.ds(at, 2 * C)]
                            nc.vector.tensor_tensor(mine, mine, accp[:, :], ALU.add).then_inc(acc_done, 1)

                        def step(lap, u):
                            onehot(lap, u, 3)
                            maximum(lap, u, 1)
                            sums(lap, u, 0)
                            add(lap, u, -2)
                        run_items(dve, step)

        def layer1_edges():
            st = ExitStack()
            with st:
                sidx = [sb(f"l1_sidx{k}", [P, TJ], I32, st) for k in range(U)]
                G = sb("l1_G", [P, U, TJ, 2 * C], F32, st)
                lo_t = sb("l1_lo", [P, U, IT], BF16, st)
                pd_t = sb("l1_pd", [P, U, 3 * C], BF16, st)
                ea_t = sb("l1_ea", [EA, U, IT], F32, st)
                sh_t = sb("l1_sh", [SH, U, IT], F32, st)
                oht = sb("l1_oht", [P, U, IT], BF16, st)
                h1_t = sb("l1_h1", [P, 2, IT], F32, st)
                a1_t = sb("l1_a1", [P, 2, IT], F32, st)
                h2_t = sb("l1_h2", [P, 2, IT], F32, st)
                a2_t = sb("l1_a2", [P, 2, IT], F32, st)
                pre_t = sb("l1_pre", [P, 2, TJ, C], F32, st)
                msg_t = sb("l1_msg", [P, U, TJ * C], F32, st)
                w_fc1 = sb("l1_fc1", [EA, C], F32, st)
                w_aw1 = sb("l1_aw1", [EA, C], F32, st)
                w_fc2 = sb("l1_fc2", [P, C], F32, st)
                w_aw2 = sb("l1_aw2", [P, C], F32, st)
                w_fc3 = sb("l1_fc3", [P, C], F32, st)
                w_sh_t = sb("l1_wsh", [SH, C], F32, st)
                w_aw3 = sb("l1_aw3", [P, HEADS], F32, st)
                cols = sb("l1_cols", [P, 4], F32, st)
                ab3_bc = sb("l1_ab3", [P, HEADS], F32, st)
                b3_row = sb("l1_b3row", [1, C], F32, st)
                b3_rest = sb("l1_b3rest", [1, C], F32, st)
                b3_cut = sb("l1_b3cut", [1, 3, C], BF16, st)
                b3_3 = sb("l1_b3", [3, TJ, C], BF16, st)
                ones3 = sb("l1_ones3", [3, P], BF16, st)
                H1 = ps("l1_H1", [P, IT], F32, st)
                A1 = ps("l1_A1", [P, IT], F32, st)
                H2 = ps("l1_H2", [P, IT], F32, st)
                A2 = ps("l1_A2", [P, IT], F32, st)
                SC = ps("l1_SC", [P, TJ, C], F32, st)
                SP_ = ps("l1_SHP", [P, TJ, C], F32, st)
                LG = ps("l1_LG", [P, TJ, HEADS], F32, st)
                s_w = sem("l1_weights", st)
                s_b3 = sem("l1_b3_loaded", st)
                s_cut = sem("l1_b3_cut", st)
                s_b3m = sem("l1_b3_moved", st)
                ld = [sem(f"l1_ld{k}", st) for k in range(U)]
                gat = [sem(f"l1_gat{k}", st) for k in range(U)]
                store = [sem(f"l1_store{k}", st) for k in range(U)]
                oht_ready = sem("l1_oht_ready", st)
                h1p = sem("l1_h1_product", st)
                a1p = sem("l1_a1_product", st)
                h2p = sem("l1_h2_product", st)
                a2p = sem("l1_a2_product", st)
                h1s = sem("l1_h1_ready", st)
                a1s = sem("l1_a1_ready", st)
                h2s = sem("l1_h2_ready", st)
                a2s = sem("l1_a2_ready", st)
                sc_ready = sem("l1_sc_ready", st)
                sh_ready = sem("l1_sh_ready", st)
                lg_ready = sem("l1_lg_ready", st)
                t_done = sem("l1_scaled", st)
                pre_ready = sem("l1_pre_ready", st)
                lg_done = sem("l1_lg_done", st)
                msg_ready = sem("l1_msg_ready", st)
                with nc.Block() as block:
                    @block.sync
                    def _(sp):
                        for t, w in ((w_fc1, fc1), (w_aw1, aw1e), (w_fc2, fc2), (w_aw2, aw2), (w_fc3, fc3),
                                     (w_sh_t, w_sh), (w_aw3, aw3)):
                            sp.dma_start(t[:, :], w).then_inc(s_w, 16)
                        for k, v in enumerate((b1, ab1, b2, ab2)):
                            sp.dma_start(cols[:, k:k + 1], v.rearrange("(p k) -> p k", k=1)).then_inc(s_w, 16)
                        sp.dma_start(ab3_bc[:, :], ab3.partition_broadcast(P)).then_inc(s_w, 16)
                        sp.dma_start(b3_row[:, :], b3.rearrange("(k c) -> k c", k=1)).then_inc(s_b3, 16)
                        sp.wait_ge(s_cut, 5)
                        for k in range(3):
                            for j in range(TJ):
                                sp.dma_start(b3_3[k:k + 1, j, :], b3_cut[0:1, k, :]).then_inc(s_b3m, 16)

                        def step(lap, u):
                            i, s, lp = item(lap, u)
                            if not exists(i, NI):
                                return
                            off = sp.value_load(items_row[0:1, bass.ds(i * 4, 1)], min_val=0, max_val=OFF_MAX)
                            row = sp.value_load(items_row[0:1, bass.ds(i * 4 + 1, 1)], min_val=0, max_val=NB * P)
                            if after(i, U):
                                hold(sp, sp_passed,
                                     (gat[s], 16 * TJ * lp),
                                     (a1p, i - U + 1),
                                     (h1p, i - U + 1),
                                     (sh_ready, i - U + 1))
                            sp.dma_start(sidx[s][:, :], src_pad[bass.ds(off, IT)].rearrange("(p j) -> p j", j=TJ)).then_inc(ld[s], 16)
                            sp.dma_start(lo_t[:, s, :], low_d[bass.ds(off, IT)].partition_broadcast(P)).then_inc(ld[s], 16)
                            sp.dma_start(pd_t[:, s, :], dst_d[1][bass.ds(row, P), :]).then_inc(ld[s], 16)
                            sp.dma_start(ea_t[:, s, :], ea32[:, bass.ds(off, IT)]).then_inc(ld[s], 16)
                            sp.dma_start(sh_t[:, s, :], ea16[:, bass.ds(off, IT)]).then_inc(ld[s], 16)
                        run_items(sp, step)

                    @block.gpsimd
                    def _(pool):
                        def step(lap, u):
                            i, s, lp = item(lap, u, 3)
                            if not exists(i, NI):
                                return
                            if after(i, U):
                                hold(pool, pool_passed,
                                     (a1p, i - U + 1),
                                     (t_done, i - U + 1))
                            hold(pool, pool_passed, (ld[s], 80 * (lp + 1)))
                            for j in range(TJ):
                                nc.gpsimd.indirect_dma_start(
                                    out=G[:, s, j, :], out_offset=None, in_=rows_d[1][:, :],
                                    in_offset=bass.IndirectOffsetOnAxis(ap=sidx[s][:, j:j + 1], axis=0)).then_inc(gat[s], 16)
                        run_items(pool, step)

                    @block.tensor
                    def _(pe):
                        pe.wait_ge(s_w, 16 * 12)
                        pe.wait_ge(s_cut, 5)
                        pe.wait_ge(s_b3m, 16 * 3 * TJ)

                        def first(lap, u, d):
                            i, s, lp = item(lap, u, d)
                            if not exists(i, NI):
                                return
                            pe.wait_ge(ld[s], 80 * (lp + 1))
                            if after(i, 1):
                                pe.wait_ge(h1s, i)
                            nc.tensor.matmul(H1[:, :], w_fc1[:, :], ea_t[:, s, :], start=True, stop=True).then_inc(h1p, 1)
                            pe.wait_ge(gat[s], 16 * TJ * (lp + 1))
                            pe.wait_ge(oht_ready, i + 1)
                            if after(i, 1):
                                pe.wait_ge(a1s, i)
                            av = A1[:, :].rearrange("p (e j) -> p j e", j=TJ)
                            for j in range(TJ):
                                nc.tensor.matmul(av[:, j, :], G[:, s, j, C:2 * C], ident[:, :], is_transpose=True,
                                                 start=(j == 0), stop=False, skip_group_check=True)
                            for k in range(3):
                                nc.tensor.matmul(A1[:, :], pd_t[:, s, k * C:(k + 1) * C], oht[:, s, :],
                                                 start=False, stop=False, skip_group_check=True)
                            nc.tensor.matmul(A1[:, :], w_aw1[:, :], ea_t[:, s, :], start=False, stop=True,
                                             skip_group_check=True).then_inc(a1p, 1)

                        def second(lap, u, d):
                            i, s, _ = item(lap, u, d)
                            if not exists(i, NI):
                                return
                            b = s % 2
                            pe.wait_ge(h1s, i + 1)
                            if after(i, 1):
                                pe.wait_ge(h2s, i)
                            nc.tensor.matmul(H2[:, :], w_fc2[:, :], h1_t[:, b, :], start=True, stop=True).then_inc(h2p, 1)
                            pe.wait_ge(a1s, i + 1)
                            if after(i, 1):
                                pe.wait_ge(a2s, i)
                            nc.tensor.matmul(A2[:, :], w_aw2[:, :], a1_t[:, b, :], start=True, stop=True).then_inc(a2p, 1)

                        def third(lap, u, d):
                            i, s, _ = item(lap, u, d)
                            if not exists(i, NI):
                                return
                            b = s % 2
                            pe.wait_ge(h2s, i + 1)
                            if after(i, 1):
                                pe.wait_ge(t_done, i)
                            nc.tensor.matmul(SC[:, :, :], ones3[:, :], b3_3[:, :, :], start=True, stop=False,
                                             skip_group_check=True)
                            hv = h2_t[:, b, :].rearrange("p (e j) -> p j e", j=TJ)
                            sv = sh_t[:, s, :].rearrange("p (e j) -> p j e", j=TJ)
                            a2v = a2_t[:, b, :].rearrange("p (e j) -> p j e", j=TJ)
                            for j in range(TJ):
                                last = nc.tensor.matmul(SC[:, j, :], hv[:, j, :], w_fc3[:, :], start=False,
                                                        stop=(j == TJ - 1), skip_group_check=True)
                            last.then_inc(sc_ready, 1)
                            if after(i, 1):
                                pe.wait_ge(pre_ready, i)
                            for j in range(TJ):
                                last = nc.tensor.matmul(SP_[:, j, :], sv[:, j, :], w_sh_t[:, :], start=True, stop=True)
                            last.then_inc(sh_ready, 1)
                            pe.wait_ge(a2s, i + 1)
                            if after(i, 1):
                                pe.wait_ge(lg_done, i)
                            for j in range(TJ):
                                last = nc.tensor.matmul(LG[:, j, :], a2v[:, j, :], w_aw3[:, :], start=True, stop=True)
                            last.then_inc(lg_ready, 1)

                        def step(lap, u):
                            first(lap, u, 2)
                            second(lap, u, 1)
                            third(lap, u, 0)
                        run_items(pe, step)

                    @block.scalar
                    def _(act):
                        act.wait_ge(s_w, 16 * 12)

                        def silu(lap, u, d, product, ready, used, out_t, in_p, col):
                            i, s, _ = item(lap, u, d)
                            if not exists(i, NI):
                                return
                            act.wait_ge(product, i + 1)
                            if after(i, 2):
                                act.wait_ge(used, i - 1)
                            nc.scalar.activation(out_t[:, s % 2, :], in_p[:, :], ACT.Silu,
                                                 bias=cols[:, col:col + 1]).then_inc(ready, 1)

                        def message(lap, u, d):
                            i, s, lp = item(lap, u, d)
                            if not exists(i, NI):
                                return
                            act.wait_ge(pre_ready, i + 1)
                            if after(i, U):
                                act.wait_ge(store[s], 16 * lp)
                            nc.scalar.activation(msg_t[:, s, :], pre_t[:, s % 2, :, :].rearrange("p j c -> p (j c)"),
                                                 ACT.Silu).then_inc(msg_ready, 1)

                        def keep(lap, u, d):
                            i, s, _ = item(lap, u, d)
                            if not exists(i, NI):
                                return
                            act.wait_ge(msg_ready, i + 1)
                            act.dma_start(msg_d[bass.ds(i, 1), :, :].rearrange("a p c -> (a p) c"),
                                          msg_t[:, s, :]).then_inc(store[s], 16)

                        def step(lap, u):
                            silu(lap, u, 2, h1p, h1s, h2p, h1_t, H1, 0)
                            silu(lap, u, 2, a1p, a1s, a2p, a1_t, A1, 1)
                            silu(lap, u, 1, h2p, h2s, sc_ready, h2_t, H2, 2)
                            silu(lap, u, 1, a2p, a2s, lg_ready, a2_t, A2, 3)
                            message(lap, u, -1)
                            keep(lap, u, -2)
                        run_items(act, step)
                        for k in range(U):
                            act.wait_ge(store[k], 16 * LAPS)

                    @block.vector
                    def _(dve):
                        dve.wait_ge(s_b3, 16)
                        nc.vector.tensor_copy(b3_cut[0:1, 0, :], b3_row[:, :]).then_inc(s_cut, 1)
                        dve.wait_ge(s_cut, 1)
                        nc.vector.tensor_tensor(b3_rest[:, :], b3_row[:, :], b3_cut[0:1, 0, :], ALU.subtract).then_inc(s_cut, 1)
                        dve.wait_ge(s_cut, 2)
                        nc.vector.tensor_copy(b3_cut[0:1, 1, :], b3_rest[:, :]).then_inc(s_cut, 1)
                        dve.wait_ge(s_cut, 3)
                        nc.vector.tensor_tensor(b3_cut[0:1, 2, :], b3_rest[:, :], b3_cut[0:1, 1, :], ALU.subtract).then_inc(s_cut, 1)
                        nc.vector.memset(ones3[:, :], 1.0).then_inc(s_cut, 1)
                        dve.wait_ge(s_w, 16 * 12)

                        def onehot(lap, u, d):
                            i, s, lp = item(lap, u, d)
                            if not exists(i, NI):
                                return
                            dve.wait_ge(ld[s], 80 * (lp + 1))
                            nc.vector.tensor_scalar(oht[:, s, :], lo_t[:, s, :], iota_col[:, 0:1], None,
                                                    ALU.is_equal).then_inc(oht_ready, 1)

                        def message(lap, u, d):
                            i, s, lp = item(lap, u, d)
                            if not exists(i, NI):
                                return
                            b = s % 2
                            dve.wait_ge(gat[s], 16 * TJ * (lp + 1))
                            dve.wait_ge(sc_ready, i + 1)
                            if after(i, 2):
                                dve.wait_ge(msg_ready, i - 1)
                            nc.vector.tensor_tensor(pre_t[:, b, :, :], G[:, s, :, 0:C], SC[:, :, :], ALU.mult).then_inc(t_done, 1)
                            dve.wait_ge(t_done, i + 1)
                            dve.wait_ge(sh_ready, i + 1)
                            nc.vector.tensor_tensor(pre_t[:, b, :, :], pre_t[:, b, :, :], SP_[:, :, :], ALU.add).then_inc(pre_ready, 1)
                            dve.wait_ge(lg_ready, i + 1)
                            mine = logits[:, bass.ds(i * (TJ * HEADS), TJ * HEADS)].rearrange("p (j h) -> p j h", h=HEADS)
                            nc.vector.tensor_tensor(mine, LG[:, :, :], ab3_bc[:, :].unsqueeze(1).to_broadcast([P, TJ, HEADS]),
                                                    ALU.add).then_inc(lg_done, 1)

                        def step(lap, u):
                            onehot(lap, u, 3)
                            message(lap, u, 0)
                        run_items(dve, step)

        def layer1_aggregate():
            T = NI * TJ
            st = ExitStack()
            with st:
                bad = sb("ag_bad", [P, T], F32, st)
                late = sb("ag_late", [P, T], F32, st)
                ex = sb("ag_ex", [P, HEADS, T], F32, st)
                alpha = sb("ag_alpha", [P, 2, T], F32, st)
                mx = sb("ag_mx", [P, HEADS], F32, st)
                mx_all = sb("ag_mx_all", [P, HEADS], F32, st)
                neg = sb("ag_neg", [P, HEADS], F32, st)
                tot = sb("ag_tot", [P, HEADS], F32, st)
                tot_all = sb("ag_tot_all", [P, HEADS], F32, st)
                share = sb("ag_share", [P, HEADS], F32, st)
                msg_t = sb("ag_msg", [P, U, TJ, C], F32, st)
                pick = sb("ag_pick", [P, 2, TJ, P], F32, st)
                accp = [ps(f"ag_accp{k}", [P, C], F32, st) for k in range(2)]
                s_chain = sem("ag_chain", st)
                s_mx = sem("ag_mx_ready", st)
                s_mxa = sem("ag_mx_all_ready", st)
                s_neg = sem("ag_neg_ready", st)
                s_ex = sem("ag_ex_ready", st)
                s_tot = sem("ag_tot_ready", st)
                ld = [sem(f"ag_ld{k}", st) for k in range(U)]
                pick_ready = sem("ag_pick_ready", st)
                accp_ready = sem("ag_accp_ready", st)
                acc_done = sem("ag_acc_done", st)
                with nc.Block() as block:
                    @block.sync
                    def _(sp):
                        def step(lap, u):
                            i, s, lp = item(lap, u)
                            if not exists(i, NI):
                                return
                            if after(i, U):
                                hold(sp, sp_passed, (accp_ready, i - U + 1))
                            sp.dma_start(msg_t[:, s, :, :], msg_d[bass.ds(i, 1), :, :].rearrange(
                                "a p (j c) -> (a p) j c", j=TJ)).then_inc(ld[s], 16)
                        run_items(sp, step)

                    @block.gpsimd
                    def _(pool):
                        pool.wait_ge(s_mx, 1)
                        nc.gpsimd.partition_all_reduce(mx_all[:, :], mx[:, :], P, RMAX).then_inc(s_mxa, 1)
                        pool.wait_ge(s_ex, HEADS)
                        nc.gpsimd.partition_all_reduce(tot_all[:, :], tot[:, :], P, RADD).then_inc(s_tot, 1)

                    @block.scalar
                    def _(act):
                        lg = logits.rearrange("p (t h) -> p h t", h=HEADS)
                        act.wait_ge(s_neg, 1)
                        for h in range(HEADS):
                            nc.scalar.activation(ex[:, h, :], lg[:, h, :], ACT.Exp, bias=neg[:, h:h + 1],
                                                 accum_out=tot[:, h:h + 1]).then_inc(s_ex, 1)

                    @block.tensor
                    def _(pe):
                        def step(lap, u):
                            i, s, lp = item(lap, u)
                            if not exists(i, NI):
                                return
                            b = s % 2
                            pe.wait_ge(ld[s], 16 * (lp + 1))
                            pe.wait_ge(pick_ready, TJ * (i + 1))
                            if after(i, 2):
                                pe.wait_ge(acc_done, i - 1)
                            for j in range(TJ):
                                last = nc.tensor.matmul(accp[b][:, :], pick[:, b, j, :], msg_t[:, s, j, :],
                                                        start=(j == 0), stop=(j == TJ - 1))
                            last.then_inc(accp_ready, 1)
                        run_items(pe, step)

                    @block.vector
                    def _(dve):
                        chain = [0]

                        def link(ins):
                            chain[0] += 1
                            ins.then_inc(s_chain, 1)
                            dve.wait_ge(s_chain, chain[0])
                        link(nc.vector.tensor_scalar(bad[:, :], local[:, :], 0.0, None, ALU.is_lt))
                        link(nc.vector.scalar_tensor_tensor(out=late[:, :], in0=local[:, :], scalar=float(P), in1=bad[:, :],
                                                            op0=ALU.is_ge, op1=ALU.add))
                        link(nc.vector.tensor_scalar(bad[:, :], late[:, :], FAR, None, ALU.mult))
                        lv = logits.rearrange("p (t h) -> p t h", h=HEADS)
                        link(nc.vector.tensor_tensor(lv, lv, bad[:, :].unsqueeze(2).to_broadcast([P, T, HEADS]), ALU.add))
                        nc.vector.tensor_reduce(mx[:, :], logits.rearrange("p (t h) -> p h t", h=HEADS), AX_X,
                                                ALU.max).then_inc(s_mx, 1)
                        dve.wait_ge(s_mxa, 1)
                        nc.vector.tensor_scalar(neg[:, :], mx_all[:, :], -1.0, None, ALU.mult).then_inc(s_neg, 1)
                        dve.wait_ge(s_tot, 1)
                        link(nc.vector.tensor_scalar(share[:, :], tot_all[:, :], float(HEADS), None, ALU.mult))
                        link(nc.vector.reciprocal(share[:, :], share[:, :]))
                        link(nc.vector.tensor_scalar(alpha[:, 0, :], ex[:, 0, :], share[:, 0:1], None, ALU.mult))
                        for h in range(1, HEADS):
                            link(nc.vector.scalar_tensor_tensor(out=alpha[:, h % 2, :], in0=ex[:, h, :],
                                                                scalar=share[:, h:h + 1], in1=alpha[:, (h - 1) % 2, :],
                                                                op0=ALU.mult, op1=ALU.add))
                        al = alpha[:, (HEADS - 1) % 2, :]
                        link(nc.vector.memset(acc1, 0.0))

                        def weigh(lap, u, d):
                            i, s, _ = item(lap, u, d)
                            if not exists(i, NI):
                                return
                            b = s % 2
                            if after(i, 2):
                                dve.wait_ge(accp_ready, i - 1)
                            for j in range(TJ):
                                nc.vector.tensor_scalar(pick[:, b, j, :], iota_row[:, :], local[:, bass.ds(i * TJ + j, 1)],
                                                        al[:, bass.ds(i * TJ + j, 1)], ALU.is_equal,
                                                        ALU.mult).then_inc(pick_ready, 1)

                        def add(lap, u, d):
                            i, s, _ = item(lap, u, d)
                            if not exists(i, NI):
                                return
                            at = dve.value_load(items_row[0:1, bass.ds(i * 4 + 1, 1)], min_val=0, max_val=NB * P)
                            dve.wait_ge(accp_ready, i + 1)
                            if after(i, 1):
                                dve.wait_ge(acc_done, i)
                            mine = acc1[:, bass.ds(at, C)]
                            nc.vector.tensor_tensor(mine, mine, accp[s % 2][:, :], ALU.add).then_inc(acc_done, 1)

                        def step(lap, u):
                            weigh(lap, u, 1)
                            add(lap, u, 0)
                        run_items(dve, step)

        def finish():
            st = ExitStack()
            with st:
                w_o = sb("fi_w", [P, C], F32, st)
                a_b = sb("fi_ab", [P, 2, C], F32, st)
                a_t = sb("fi_at", [P, 2, C], F32, st)
                stats = sb("fi_stats", [P, 3, NBT], F32, st)
                O = sb("fi_O", [P, NBT, C], F32, st)
                tp = [ps(f"fi_tp{k}", [P, C], F32, st) for k in range(2)]
                pp = [ps(f"fi_pp{k}", [P, C], F32, st) for k in range(2)]
                s_in = sem("fi_in", st)
                s_chain = sem("fi_chain", st)
                s_var = sem("fi_var", st)
                s_root = sem("fi_root", st)
                s_tp = sem("fi_tp_ready", st)
                s_ab = sem("fi_ab_ready", st)
                s_at = sem("fi_at_ready", st)
                s_pp = sem("fi_pp_ready", st)
                s_sum = sem("fi_sum", st)
                s_fin = sem("fi_fin", st)
                s_out = sem("fi_out", st)
                with nc.Block() as block:
                    @block.sync
                    def _(sp):
                        sp.dma_start(w_o[:, :], w_out).then_inc(s_in, 16)
                        sp.wait_ge(s_fin, 1)
                        full = N // P
                        sp.dma_start(out[0:full * P, :].rearrange("(n p) c -> p n c", p=P), O[:, 0:full, :]).then_inc(s_out, 16)
                        sp.dma_start(out[full * P:N, :], O[0:N - full * P, full, :]).then_inc(s_out, 16)
                        sp.wait_ge(s_out, 32)

                    @block.tensor
                    def _(pe):
                        pe.wait_ge(s_in, 16)

                        def step(lap, u):
                            i, s, _ = item(lap, u, 1, 2)
                            if exists(i, NBT):
                                if after(i, 2):
                                    pe.wait_ge(s_at, i - 1)
                                pe.wait_ge(s_ab, i + 1)
                                nc.tensor.transpose(tp[s][:, :], a_b[:, s, :], ident[:, :]).then_inc(s_tp, 1)
                            i, s, _ = item(lap, u, 0, 2)
                            if exists(i, NBT):
                                pe.wait_ge(s_at, i + 1)
                                if after(i, 2):
                                    pe.wait_ge(s_sum, i - 1)
                                nc.tensor.matmul(pp[s][:, :], a_t[:, s, :], w_o[:, :], start=True, stop=True).then_inc(s_pp, 1)
                        run_items(pe, step, NBT // 2, 2)

                    @block.gpsimd
                    def _(pool):
                        def step(lap, u):
                            i, s, _ = item(lap, u, 0, 2)
                            if not exists(i, NBT):
                                return
                            if after(i, 2):
                                pool.wait_ge(s_tp, i - 1)
                            nc.gpsimd.tensor_copy(a_b[:, s, :], acc1[:, bass.ds(i * C, C)]).then_inc(s_ab, 1)
                        run_items(pool, step, NBT // 2, 2)

                    @block.scalar
                    def _(act):
                        def step(lap, u):
                            i, s, _ = item(lap, u, 0, 2)
                            if not exists(i, NBT):
                                return
                            act.wait_ge(s_tp, i + 1)
                            if after(i, 2):
                                act.wait_ge(s_pp, i - 1)
                            nc.scalar.activation(a_t[:, s, :], tp[s][:, :], ACT.Copy).then_inc(s_at, 1)
                        run_items(act, step, NBT // 2, 2)
                        norm_scalar(act, stats, s_var, s_root)

                    @block.vector
                    def _(dve):
                        def step(lap, u):
                            i, s, _ = item(lap, u, 0, 2)
                            if not exists(i, NBT):
                                return
                            dve.wait_ge(s_pp, i + 1)
                            mine = H[:, bass.ds(i, 1), :].rearrange("p n c -> p (n c)")
                            nc.vector.tensor_tensor(mine, mine, pp[s][:, :], ALU.add).then_inc(s_sum, 1)
                        run_items(dve, step, NBT // 2, 2)
                        dve.wait_ge(s_sum, NBT)
                        norm_vector(dve, [s_chain, 0], H[:, :, :], s_var, s_root, stats, O[:, :, :], False)
                        nc.vector.tensor_tensor(O[:, :, :], O[:, :, :], X[:, :, :], ALU.add).then_inc(s_fin, 1)

        index_pass()
        node_tables(0, w0cat, b0cat)
        layer0_edges()
        node_tables(1, w1cat, None)
        layer1_edges()
        layer1_aggregate()
        finish()


def kernel(x, src, dst, edge_attr_16, edge_attr_32, L0_gnn_W_src, L0_gnn_b_src, L0_gnn_W_dst, L0_gnn_b_dst,
           L0_gnn_W_v, L0_gnn_b_v, L1_gnn_W_node, L1_gnn_fc1, L1_gnn_b1, L1_gnn_fc2, L1_gnn_b2, L1_gnn_fc3,
           L1_gnn_b3, L1_gnn_W_sh, L1_gnn_aW1, L1_gnn_ab1, L1_gnn_aW2, L1_gnn_ab2, L1_gnn_aW3, L1_gnn_ab3,
           L1_gnn_W_out):
    import numpy as np
    import concourse.bacc as bacc
    from concourse.bass_utils import run_bass_kernel_spmd

    def pad(a, shape, at, fill=0):
        a = np.asarray(a)
        full = np.full(shape, fill, a.dtype)
        full[tuple(slice(o, o + n) for o, n in zip(at, a.shape))] = a
        return full
    aW1 = np.asarray(L1_gnn_aW1)
    half = C // 2
    dst_pad = pad(dst, (EP + 2,), (1,), NO_NODE)
    dst_pad[0] = -1
    laid = {
        "x": pad(x, (NP, C), (0, 0)),
        "src_pad": pad(src, (EP,), (0,)),
        "dst_pad": dst_pad,
        "ea32": pad(np.asarray(edge_attr_32).T, (EA, EP), (0, 0)),
        "ea16": pad(np.asarray(edge_attr_16).T, (SH, EP), (0, 0)),
        "w0cat": np.concatenate([np.asarray(w).T for w in (L0_gnn_W_src, L0_gnn_W_v, L0_gnn_W_dst)], axis=1),
        "b0cat": np.concatenate([np.asarray(b) for b in (L0_gnn_b_src, L0_gnn_b_v, L0_gnn_b_dst)]),
        "w1cat": np.concatenate([np.asarray(L1_gnn_W_node), pad(aW1[0:half], (C, C), (0, 0)),
                                 pad(aW1[half:2 * half], (C, C), (0, 0))], axis=1),
        "fc1": L1_gnn_fc1, "b1": L1_gnn_b1, "fc2": L1_gnn_fc2, "b2": L1_gnn_b2, "fc3": L1_gnn_fc3,
        "b3": L1_gnn_b3, "w_sh": L1_gnn_W_sh, "aw1e": aW1[2 * half:], "ab1": L1_gnn_ab1, "aw2": L1_gnn_aW2,
        "ab2": L1_gnn_ab2, "aw3": L1_gnn_aW3, "ab3": L1_gnn_ab3, "w_out": L1_gnn_W_out,
    }
    nc = bacc.Bacc("TRN2", target_bir_lowering=False, num_devices=1)
    arrays, args = {}, []
    for name, a in laid.items():
        a = np.ascontiguousarray(a)
        arrays[f"in_{name}_dram"] = a
        args.append(nc.dram_tensor(f"in_{name}_dram", a.shape, mybir.dt.from_np(a.dtype), kind="ExternalInput").ap())
    args.append(nc.dram_tensor("out_dram", (N, C), F32, kind="ExternalOutput").ap())
    build(nc, *args)
    r = run_bass_kernel_spmd(nc, [arrays], core_ids=[0])
    return r.results[0]["out_dram"]
```

```python
from contextlib import ExitStack

import concourse.bass as bass
from concourse import mybir

F32 = mybir.dt.float32
BF16 = mybir.dt.bfloat16
I32 = mybir.dt.int32
ALU = mybir.AluOpType
ACT = mybir.ActivationFunctionType
AX_X = mybir.AxisListType.X
RMAX = bass.bass_isa.ReduceOp.max
RADD = bass.bass_isa.ReduceOp.add

P = 128
N = 6250
E = 106250
C = 128
NB = -(-N // P)
NBT = NB + 1
NP = NBT * P
IT = 512
TJ = IT // P
NI = (E + NB * (IT - 1)) // IT
OFF_MAX = -(-E // IT) * IT
EQ = -(-(OFF_MAX + IT) // P)
EP = EQ * P
SEL_DVE = 3
HEADS = 8
EA = 32
SH = 16
SLOPE = 0.2
EPS = 1e-5
FAR = -3.0e38
NO_NODE = 8191
OFF_RANGE = 16384.0
U = 8
R = 4
LAPS = NI // U
assert NI % U == 0 and NBT % 2 == 0 and (OFF_MAX + IT) <= EP


def item(lap, u, d=0, turn=U):
    v = u + d
    return (lap + v // turn) * turn + v % turn, v % turn, lap + v // turn


def after(i, n):
    return not isinstance(i, int) or i >= n


def ring(s, lap):
    return s % R, lap * (U // R) + s // R


def exists(i, count):
    return not isinstance(i, int) or 0 <= i < count


def hold(eng, passed, *waits):
    for sem, n in waits:
        eng.wait_ge(sem, n)
        eng.sem_inc(passed, 1)


def run_items(eng, step, turns=LAPS, turn=U):
    for lap in (-1, 0):
        for u in range(turn):
            step(lap, u)
    with eng.Fori(1, turns - 1) as lap:
        for u in range(turn):
            step(lap, u)
    for lap in (turns - 1, turns):
        for u in range(turn):
            step(lap, u)


def build(nc, x, src_pad, dst_pad, ea32, ea16, w0cat, b0cat, w1cat, fc1, b1, fc2, b2, fc3, b3, w_sh,
          aw1e, ab1, aw2, ab2, aw3, ab3, w_out, out):
    top = ExitStack()
    with top:
        def sb(name, shape, dt, stack=top):
            return stack.enter_context(nc.sbuf_tensor(name, shape, dt))

        def ps(name, shape, dt=F32, stack=top):
            return stack.enter_context(nc.psum_tensor(name, shape, dt))

        def sem(name, stack=top):
            return stack.enter_context(nc.semaphore(name))

        sp_passed = sem("sp_passed")
        pool_passed = sem("pool_passed")

        def dram(name, shape, dt):
            return nc.dram_tensor(name, shape, dt).ap()

        pen_d = dram("pen_d", [EP], BF16)
        low_d = dram("low_d", [EP], BF16)
        pair_d = dram("pair_d", [EP, 2], F32)
        items_d = dram("items_d", [NI, 4], I32)
        base_d = dram("base_d", [NI], F32)
        rows_d = [dram(f"rows{l}_d", [NP, 2 * C], F32) for l in range(2)]
        dst_d = [dram(f"dst{l}_d", [NP, 3 * C], BF16) for l in range(2)]
        ea_d = dram("ea_d", [3 * EA, EP], BF16)
        sh_d = dram("sh_d", [3 * SH, EP], BF16)
        msg_d = dram("msg_d", [NI, P, TJ * C], F32)

        ident = sb("ident", [P, P], F32)
        iota_row = sb("iota_row", [P, P], F32)
        iota_col = sb("iota_col", [P, 2], F32)
        items_row = sb("items_row", [1, NI * 4], I32)
        base_bc = sb("base_bc", [P, NI], F32)
        local = sb("local", [P, NI * TJ], F32)
        X = sb("X", [P, NBT, C], F32)
        H = sb("H", [P, NBT, C], F32)
        big = sb("big", [P, NBT * 2 * C + NI * TJ * HEADS // 4], F32)
        acc0 = big[:, 0:NBT * 2 * C]
        acc1 = big[:, 0:NBT * C]
        logits = big[:, NBT * C:NBT * C + NI * TJ * HEADS]
        scratch = big[:, 0:NBT * C].rearrange("p (n c) -> p n c", c=C)
        assert NBT * C + NI * TJ * HEADS <= big.shape[1]

        x_v = x.rearrange("(n p) c -> p n c", p=P)


        def norm_vector(eng, chain, source, to_act, from_act, stats, target, relu):
            def link(ins):
                chain[1] += 1
                ins.then_inc(chain[0], 1)
                eng.wait_ge(chain[0], chain[1])
            mean, var, rstd = (stats[:, k, :] for k in range(3))

            def wide(v):
                return v.unsqueeze(2).to_broadcast([P, NBT, C])
            link(nc.vector.tensor_reduce(mean, source, AX_X, ALU.add))
            link(nc.vector.tensor_scalar(mean, mean, 1.0 / C, None, ALU.mult))
            link(nc.vector.tensor_tensor(target, source, wide(mean), ALU.subtract))
            link(nc.vector.tensor_tensor(scratch, target, target, ALU.mult))
            link(nc.vector.tensor_reduce(var, scratch, AX_X, ALU.add))
            nc.vector.tensor_scalar(var, var, 1.0 / C, EPS, ALU.mult, ALU.add).then_inc(to_act, 1)
            eng.wait_ge(from_act, 1)
            link(nc.vector.reciprocal(rstd, rstd))
            if relu:
                link(nc.vector.scalar_tensor_tensor(out=target, in0=target, scalar=0.0, in1=wide(rstd),
                                                    op0=ALU.max, op1=ALU.mult))
            else:
                link(nc.vector.tensor_tensor(target, target, wide(rstd), ALU.mult))

        def norm_scalar(eng, stats, to_act, from_act):
            eng.wait_ge(to_act, 1)
            nc.scalar.activation(stats[:, 2, :], stats[:, 1, :], ACT.Sqrt).then_inc(from_act, 1)

        def index_pass():
            st = ExitStack()
            with st:
                before = sb("before", [P, EQ], I32, st)
                here = sb("here", [P, EQ], I32, st)
                behind = sb("behind", [P, EQ], I32, st)
                here_f = sb("here_f", [P, EQ], F32, st)
                flag = sb("flag", [P, EQ], F32, st)
                pen = sb("pen", [P, EQ], BF16, st)
                low_i = sb("low_i", [P, EQ], I32, st)
                low = sb("low", [P, EQ], BF16, st)
                pair = sb("pair", [P, EQ, 2], F32, st)
                junk = sb("junk", [P, EQ], BF16, st)
                count = sb("count", [P, NBT], F32, st)
                ones = sb("ones", [P, P], F32, st)
                first = sb("first", [P, NBT], F32, st)
                row = sb("row", [P, 8, NB], F32, st)
                tiles_i = sb("tiles_i", [P, NB], I32, st)
                pick = sb("pick", [P, 8], F32, st)
                table = sb("table", [P, 2, 4], I32, st)
                base = sb("base", [P, 2], F32, st)
                total = ps("total", [P, NBT], F32, st)
                s_in = sem("ip_in", st)
                s_const = sem("ip_const", st)
                s_chain = sem("ip_chain", st)
                s_rows = sem("ip_rows", st)
                s_count = sem("ip_count", st)
                s_total = sem("ip_total", st)
                s_table = sem("ip_table", st)
                s_out = sem("ip_out", st)
                s_items = sem("ip_items", st)
                s_back = sem("ip_back", st)
                with nc.Block() as block:
                    @block.sync
                    def _(sp):
                        for k, t in enumerate((before, here, behind)):
                            sp.dma_start(t[:, :], dst_pad[k:k + EP].rearrange("(p q) -> p q", q=EQ)).then_inc(s_in, 16)
                        sp.wait_ge(s_rows, 3)
                        sp.dma_start(pen_d.rearrange("(p q) -> p q", q=EQ), pen[:, :]).then_inc(s_out, 16)
                        sp.dma_start(low_d.rearrange("(p q) -> p q", q=EQ), low[:, :]).then_inc(s_out, 16)
                        sp.dma_start(pair_d.rearrange("(p q) k -> p q k", q=EQ), pair[:, :, :]).then_inc(s_out, 16)
                        sp.wait_ge(s_table, 2)
                        for g in range(2):
                            sp.dma_start(items_d[g * P:(g + 1) * P, :], table[:, g, :]).then_inc(s_items, 16)
                            sp.dma_start(base_d[g * P:(g + 1) * P].rearrange("(p k) -> p k", k=1),
                                         base[:, g:g + 1]).then_inc(s_items, 16)
                        sp.wait_ge(s_items, 64)
                        sp.dma_start(items_row[:, :], items_d.rearrange("(a i) k -> a (i k)", a=1)).then_inc(s_back, 16)
                        sp.dma_start(base_bc[:, :], base_d.partition_broadcast(P)).then_inc(s_back, 16)
                        sp.wait_ge(s_back, 32)
                        sp.wait_ge(s_out, 48)

                    @block.gpsimd
                    def _(pool):
                        nc.gpsimd.memset(ident[:, :], 0.0).then_inc(s_const, 1)
                        pool.wait_ge(s_const, 1)
                        nc.gpsimd.affine_select(out=ident[:, :], in_=ident[:, :], compare_op=ALU.not_equal, fill=1.0,
                                                base=0, pattern=[[-1, P]], channel_multiplier=1).then_inc(s_const, 1)
                        nc.gpsimd.iota(iota_row[:, :], [[1, P]], base=0, channel_multiplier=0,
                                       allow_small_or_imprecise_dtypes=True).then_inc(s_const, 1)
                        nc.gpsimd.iota(iota_col[:, :], [[P, 2]], base=0, channel_multiplier=1,
                                       allow_small_or_imprecise_dtypes=True).then_inc(s_const, 1)
                        nc.gpsimd.memset(ones[:, :], 1.0).then_inc(s_const, 1)
                        nc.gpsimd.memset(table[:, :, :], 0).then_inc(s_const, 1)

                    @block.tensor
                    def _(pe):
                        pe.wait_ge(s_const, 6)
                        pe.wait_ge(s_count, NBT)
                        nc.tensor.matmul(total[:, :], ones[:, :], count[:, :], start=True, stop=True).then_inc(s_total, 1)

                    @block.vector
                    def _(dve):
                        chain = [0]

                        def link(ins):
                            chain[0] += 1
                            ins.then_inc(s_chain, 1)
                            dve.wait_ge(s_chain, chain[0])
                        dve.wait_ge(s_in, 48)
                        link(nc.vector.tensor_tensor(flag[:, :], here[:, :], before[:, :], ALU.not_equal))
                        nc.vector.tensor_scalar(pen[:, :], flag[:, :], FAR, None, ALU.mult).then_inc(s_rows, 1)
                        link(nc.vector.tensor_scalar(low_i[:, :], here[:, :], P - 1, None, ALU.bitwise_and))
                        nc.vector.tensor_copy(low[:, :], low_i[:, :]).then_inc(s_rows, 1)
                        link(nc.vector.tensor_copy(here_f[:, :], here[:, :]))
                        nc.vector.tensor_copy(pair[:, :, 0], here_f[:, :])
                        link(nc.vector.tensor_tensor(flag[:, :], here[:, :], behind[:, :], ALU.is_equal))
                        nc.vector.scalar_tensor_tensor(out=pair[:, :, 1], in0=flag[:, :], scalar=OFF_RANGE,
                                                       in1=here_f[:, :], op0=ALU.mult, op1=ALU.add).then_inc(s_rows, 1)
                        for b in range(NBT):
                            if b:
                                dve.wait_ge(s_count, b)
                            nc.vector.tensor_scalar(junk[:, :], here_f[:, :], float(P * b), 0.0, ALU.is_lt,
                                                    ALU.add, accum_out=count[:, b:b + 1]).then_inc(s_count, 1)
                        dve.wait_ge(s_total, 1)
                        link(nc.vector.tensor_copy(first[:, :], total[:, :]))
                        n_up, tiles, incl, excl, q0, ge, gx, zero = (row[:, k, :] for k in range(8))
                        link(nc.vector.tensor_tensor(n_up, first[:, 1:NBT], first[:, 0:NB], ALU.subtract))
                        link(nc.vector.tensor_scalar(tiles_i[:, :], n_up, float(IT - 1), None, ALU.add))
                        link(nc.vector.tensor_scalar(tiles_i[:, :], tiles_i[:, :], IT.bit_length() - 1, None,
                                                     ALU.arith_shift_right))
                        link(nc.vector.tensor_copy(tiles, tiles_i[:, :]))
                        link(nc.vector.memset(zero, 0.0))
                        link(nc.vector.tensor_tensor_scan(incl, zero, tiles, 0.0, ALU.add, ALU.add))
                        link(nc.vector.tensor_tensor(excl, incl, tiles, ALU.subtract))
                        link(nc.vector.scalar_tensor_tensor(out=q0, in0=excl, scalar=-float(IT), in1=first[:, 0:NB],
                                                            op0=ALU.mult, op1=ALU.add))
                        dve.wait_ge(s_const, 6)
                        for g in range(2):
                            me = iota_col[:, g:g + 1]
                            nb, off = pick[:, 4 * g:4 * g + 1], pick[:, 4 * g + 1:4 * g + 2]
                            link(nc.vector.tensor_scalar(ge, incl, me, None, ALU.is_le))
                            link(nc.vector.tensor_scalar(gx, excl, me, None, ALU.is_le))
                            link(nc.vector.tensor_reduce(nb, ge, AX_X, ALU.add))
                            link(nc.vector.tensor_tensor(gx, gx, ge, ALU.subtract))
                            link(nc.vector.tensor_tensor(gx, gx, q0, ALU.mult))
                            link(nc.vector.tensor_reduce(off, gx, AX_X, ALU.add))
                            link(nc.vector.scalar_tensor_tensor(out=off, in0=me, scalar=float(IT), in1=off,
                                                                op0=ALU.mult, op1=ALU.add))
                            link(nc.vector.tensor_scalar(table[:, g, 0:1], off, float(OFF_MAX), None, ALU.min))
                            link(nc.vector.tensor_scalar(table[:, g, 1:2], nb, float(P), None, ALU.mult))
                            link(nc.vector.tensor_scalar(table[:, g, 2:3], nb, float(2 * C), None, ALU.mult))
                            nc.vector.tensor_scalar(base[:, g:g + 1], nb, float(P), None, ALU.mult).then_inc(s_table, 1)

        def split_attributes():
            cols = EP // (P // SH) // 8
            chunks = []
            for a, d, k in ((ea32, ea_d, EA), (ea16, sh_d, SH)):
                q = P // k
                av = a.rearrange("c (q k) -> (c q) k", q=q)
                dv = [d[m * k:(m + 1) * k, :].rearrange("c (q k) -> (c q) k", q=q) for m in range(3)]
                for o in range(0, EP // q, cols):
                    chunks.append((av[:, o:o + cols], [v[:, o:o + cols] for v in dv]))
            slots = 3
            st = ExitStack()
            with st:
                whole = sb("sa_x", [P, slots, cols], F32, st)
                part = sb("sa_part", [P, slots, 3, cols], BF16, st)
                s_load = [sem(f"sa_load{k}", st) for k in range(slots)]
                s_store = [sem(f"sa_store{k}", st) for k in range(slots)]
                s_one = sem("sa_one", st)
                s_rest = sem("sa_rest", st)
                s_two = sem("sa_two", st)
                s_three = sem("sa_three", st)
                with nc.Block() as block:
                    @block.sync
                    def _(sp):
                        def load(n):
                            if n >= slots:
                                sp.wait_ge(s_three, n - slots + 1)
                            sp.dma_start(whole[:, n % slots, :], chunks[n][0]).then_inc(s_load[n % slots], 16)

                        def store(n):
                            sp.wait_ge(s_two, n + 1)
                            sp.wait_ge(s_three, n + 1)
                            for m in range(3):
                                sp.dma_start(chunks[n][1][m], part[:, n % slots, m, :]).then_inc(s_store[n % slots], 16)
                        for n in range(slots - 1):
                            load(n)
                        for n in range(len(chunks)):
                            if n + slots - 1 < len(chunks):
                                load(n + slots - 1)
                            store(n)
                        for k in range(slots):
                            sp.wait_ge(s_store[k], 48 * (len(chunks) // slots))

                    @block.scalar
                    def _(act):
                        def one(n):
                            k = n % slots
                            act.wait_ge(s_load[k], 16 * (n // slots + 1))
                            if n >= slots:
                                act.wait_ge(s_store[k], 48 * (n // slots))
                            nc.scalar.activation(part[:, k, 0, :], whole[:, k, :], ACT.Copy).then_inc(s_one, 1)

                        one(0)
                        for n in range(len(chunks)):
                            if n + 1 < len(chunks):
                                one(n + 1)
                            act.wait_ge(s_rest, n + 1)
                            nc.scalar.activation(part[:, n % slots, 1, :], whole[:, n % slots, :], ACT.Copy).then_inc(s_two, 1)

                    @block.vector
                    def _(dve):
                        def rest(n):
                            x_ = whole[:, n % slots, :]
                            dve.wait_ge(s_one, n + 1)
                            nc.vector.tensor_tensor(x_, x_, part[:, n % slots, 0, :], ALU.subtract).then_inc(s_rest, 1)

                        rest(0)
                        for n in range(len(chunks)):
                            if n + 1 < len(chunks):
                                rest(n + 1)
                            k = n % slots
                            dve.wait_ge(s_two, n + 1)
                            nc.vector.tensor_tensor(part[:, k, 2, :], whole[:, k, :], part[:, k, 1, :],
                                                    ALU.subtract).then_inc(s_three, 1)

        def node_tables(layer, w_dram, bias_dram):
            st = ExitStack()
            with st:
                pre = f"n{layer}_"
                wcat = sb(pre + "wcat", [P, 3 * C], F32, st)
                bias = sb(pre + "bias", [P, 3 * C], F32, st)
                stats = sb(pre + "stats", [P, 3, NBT], F32, st)
                h_b = sb(pre + "h_b", [P, 2, C], F32, st)
                h_t = sb(pre + "h_t", [P, 2, C], F32, st)
                row = sb(pre + "row", [P, 2, 3 * C], F32, st)
                rest = sb(pre + "rest", [P, 2, C], F32, st)
                split = sb(pre + "split", [P, 2, 3 * C], BF16, st)
                tp = [ps(pre + f"tp{k}", [P, C], F32, st) for k in range(2)]
                pp = [ps(pre + f"pp{k}", [P, 3 * C], F32, st) for k in range(2)]
                s_in = sem(pre + "in", st)
                s_x = sem(pre + "x", st)
                s_chain = sem(pre + "chain", st)
                s_var = sem(pre + "var", st)
                s_root = sem(pre + "root", st)
                s_h = sem(pre + "h", st)
                s_hb = sem(pre + "hb_ready", st)
                s_tp = sem(pre + "tp_ready", st)
                s_ht = sem(pre + "ht_ready", st)
                s_pp = sem(pre + "pp_ready", st)
                s_row = sem(pre + "row_ready", st)
                s_split = sem(pre + "split_ready", st)
                s_step = sem(pre + "split_step", st)
                s_store = [sem(pre + f"store{k}", st) for k in range(2)]
                with nc.Block() as block:
                    @block.sync
                    def _(sp):
                        if layer == 0:
                            for k in range(2):
                                a, b = k * NBT // 2, (k + 1) * NBT // 2
                                sp.dma_start(X[:, a:b, :], x_v[:, a:b, :]).then_inc(s_x, 16)
                        sp.dma_start(wcat[:, :], w_dram).then_inc(s_in, 16)
                        if bias_dram is not None:
                            sp.dma_start(bias[:, :], bias_dram.partition_broadcast(P)).then_inc(s_in, 16)

                        def step(lap, u):
                            i, s, _ = item(lap, u, 0, 2)
                            if not exists(i, NBT):
                                return
                            sp.wait_ge(s_row, i + 1)
                            sp.dma_start(rows_d[layer][bass.ds(i * P, P), :], row[:, s, 0:2 * C]).then_inc(s_store[s], 16)
                            sp.wait_ge(s_split, i + 1)
                            sp.dma_start(dst_d[layer][bass.ds(i * P, P), :], split[:, s, :]).then_inc(s_store[s], 16)
                        run_items(sp, step, NBT // 2, 2)
                        for k in range(2):
                            sp.wait_ge(s_store[k], 32 * (NBT // 2))

                    @block.tensor
                    def _(pe):
                        pe.wait_ge(s_in, 16 if bias_dram is None else 32)

                        def step(lap, u):
                            i, s, _ = item(lap, u, 1, 2)
                            if exists(i, NBT):
                                if after(i, 2):
                                    pe.wait_ge(s_ht, i - 1)
                                pe.wait_ge(s_hb, i + 1)
                                nc.tensor.transpose(tp[s][:, :], h_b[:, s, :], ident[:, :]).then_inc(s_tp, 1)
                            i, s, _ = item(lap, u, 0, 2)
                            if exists(i, NBT):
                                pe.wait_ge(s_ht, i + 1)
                                if after(i, 2):
                                    pe.wait_ge(s_row, i - 1)
                                nc.tensor.matmul(pp[s][:, :], h_t[:, s, :], wcat[:, :], start=True,
                                                 stop=True).then_inc(s_pp, 1)
                        run_items(pe, step, NBT // 2, 2)

                    @block.gpsimd
                    def _(pool):
                        pool.wait_ge(s_h, 1)

                        def step(lap, u):
                            i, s, _ = item(lap, u, 0, 2)
                            if not exists(i, NBT):
                                return
                            if after(i, 2):
                                pool.wait_ge(s_tp, i - 1)
                            nc.gpsimd.tensor_copy(h_b[:, s, :], H[:, bass.ds(i, 1), :].rearrange("p n c -> p (n c)")).then_inc(s_hb, 1)
                        run_items(pool, step, NBT // 2, 2)

                    @block.scalar
                    def _(act):
                        norm_scalar(act, stats, s_var, s_root)

                        def step(lap, u):
                            i, s, _ = item(lap, u, 0, 2)
                            if not exists(i, NBT):
                                return
                            act.wait_ge(s_tp, i + 1)
                            if after(i, 2):
                                act.wait_ge(s_pp, i - 1)
                            nc.scalar.activation(h_t[:, s, :], tp[s][:, :], ACT.Copy).then_inc(s_ht, 1)
                        run_items(act, step, NBT // 2, 2)

                    @block.vector
                    def _(dve):
                        chain = [s_chain, 0]
                        if layer == 0:
                            dve.wait_ge(s_x, 32)
                        else:
                            for n in range(NBT):
                                w = acc0[:, n * 2 * C:n * 2 * C + C]
                                v = acc0[:, n * 2 * C + C:(n + 1) * 2 * C]
                                nc.vector.tensor_scalar(w, w, 0.5, None, ALU.max).then_inc(s_chain, 1)
                            dve.wait_ge(s_chain, NBT)
                            for n in range(NBT):
                                w = acc0[:, n * 2 * C:n * 2 * C + C]
                                nc.vector.reciprocal(w, w).then_inc(s_chain, 1)
                            dve.wait_ge(s_chain, 2 * NBT)
                            for n in range(NBT):
                                w = acc0[:, n * 2 * C:n * 2 * C + C]
                                v = acc0[:, n * 2 * C + C:(n + 1) * 2 * C]
                                nc.vector.tensor_tensor(w, w, v, ALU.mult).then_inc(s_chain, 1)
                            dve.wait_ge(s_chain, 3 * NBT)
                            for n in range(NBT):
                                w = acc0[:, n * 2 * C:n * 2 * C + C]
                                nc.vector.tensor_tensor(X[:, n, :], X[:, n, :], w, ALU.add).then_inc(s_chain, 1)
                            dve.wait_ge(s_chain, 4 * NBT)
                            chain[1] = 4 * NBT
                        norm_vector(dve, chain, X[:, :, :], s_var, s_root, stats, H[:, :, :], True)
                        nc.vector.tensor_copy(stats[:, 0, 0:1], stats[:, 0, 0:1]).then_inc(s_h, 1)
                        if bias_dram is not None:
                            dve.wait_ge(s_in, 32)

                        def step(lap, u):
                            i, s, _ = item(lap, u, 0, 2)
                            if not exists(i, NBT):
                                return
                            dve.wait_ge(s_pp, i + 1)
                            if after(i, 2):
                                dve.wait_ge(s_store[s], 32 * item(lap, u, 0, 2)[2])
                            if bias_dram is None:
                                nc.vector.tensor_copy(row[:, s, :], pp[s][:, :]).then_inc(s_row, 1)
                            else:
                                nc.vector.tensor_tensor(row[:, s, :], pp[s][:, :], bias[:, :], ALU.add).then_inc(s_row, 1)
                            dve.wait_ge(s_row, i + 1)
                            part = row[:, s, 2 * C:3 * C]
                            hi, mid, lo = (split[:, s, k * C:(k + 1) * C] for k in range(3))
                            nc.vector.tensor_copy(hi, part).then_inc(s_step, 1)
                            dve.wait_ge(s_step, i * 3 + 1)
                            nc.vector.tensor_tensor(rest[:, s, :], part, hi, ALU.subtract).then_inc(s_step, 1)
                            dve.wait_ge(s_step, i * 3 + 2)
                            nc.vector.tensor_copy(mid, rest[:, s, :]).then_inc(s_step, 1)
                            dve.wait_ge(s_step, i * 3 + 3)
                            nc.vector.tensor_tensor(lo, rest[:, s, :], mid, ALU.subtract).then_inc(s_split, 1)
                        run_items(dve, step, NBT // 2, 2)

        def layer0_edges():
            st = ExitStack()
            with st:
                sidx = [sb(f"l0_sidx{k}", [P, TJ], I32, st) for k in range(U)]
                G = sb("l0_G", [P, R, TJ, 2 * C], F32, st)
                lo_t = sb("l0_lo", [P, R, IT], BF16, st)
                pen_t = sb("l0_pen", [P, R, IT], BF16, st)
                fd_t = sb("l0_fd", [P, R, 3 * C], BF16, st)
                pair_t = sb("l0_pair", [P, R, TJ, 2], F32, st)
                ends_t = sb("l0_ends", [P, U, TJ], F32, st)
                oht = sb("l0_oht", [P, R, IT], BF16, st)
                e_t = sb("l0_e", [P, R, IT + 1], F32, st)
                q_t = sb("l0_q", [P, 2, IT], F32, st)
                w_t = sb("l0_w", [P, 2, IT], F32, st)
                c_t = sb("l0_c", [P, 2, IT], F32, st)
                wv_t = sb("l0_wv", [P, 2, IT], F32, st)
                s_t = sb("l0_s", [P, 2, IT], F32, st)
                r_t = sb("l0_r", [P, 2, IT], F32, st)
                sel = sb("l0_sel", [P, 2, TJ, P], F32, st)
                sr_e = sb("l0_sre", [P, 2, TJ, 2 * C], F32, st)
                A = [ps(f"l0_A{k}", [P, IT], F32, st) for k in range(2)]
                V = [ps(f"l0_V{k}", [P, IT], F32, st) for k in range(2)]
                sr_p = [ps(f"l0_srp{k}", [P, 2, 2 * C], F32, st) for k in range(2)]
                accp = ps("l0_accp", [P, 2 * C], F32, st)
                ldi = [sem(f"l0_ldi{k}", st) for k in range(U)]
                ld = [sem(f"l0_ld{k}", st) for k in range(R)]
                gat = [sem(f"l0_gat{k}", st) for k in range(R)]
                oht_ready = sem("l0_oht_ready", st)
                pairs_done = sem("l0_pairs_done", st)
                a_ready = sem("l0_a_ready", st)
                v_ready = sem("l0_v_ready", st)
                a_copied = sem("l0_a_copied", st)
                e_ready = sem("l0_e_ready", st)
                carry_ready = sem("l0_carry_ready", st)
                q_ready = sem("l0_q_ready", st)
                gap_ready = sem("l0_gap_ready", st)
                up_ready = sem("l0_up_ready", st)
                down_ready = sem("l0_down_ready", st)
                w_ready = sem("l0_w_ready", st)
                c_ready = sem("l0_c_ready", st)
                wv_ready = sem("l0_wv_ready", st)
                s_ready = sem("l0_s_ready", st)
                r_ready = sem("l0_r_ready", st)
                srt_ready = sem("l0_srt_ready", st)
                sre_ready = sem("l0_sre_ready", st)
                sel_pool = sem("l0_sel_pool", st)
                sel_dve = sem("l0_sel_dve", st)
                accp_ready = sem("l0_accp_ready", st)
                acc_done = sem("l0_acc_done", st)
                zeroed = sem("l0_zeroed", st)
                with nc.Block() as block:
                    @block.sync
                    def _(sp):
                        def indices(lap, u, d):
                            i, s, lp = item(lap, u, d)
                            if not exists(i, NI):
                                return
                            off = sp.value_load(items_row[0:1, bass.ds(i * 4, 1)], min_val=0, max_val=OFF_MAX)
                            g, gl = ring(s, lp)
                            if after(i, U):
                                hold(sp, sp_passed, (gat[g], 16 * TJ * (gl + 1 - U // R)))
                            sp.dma_start(sidx[s][:, :], src_pad[bass.ds(off, IT)].rearrange("(p j) -> p j", j=TJ)).then_inc(ldi[s], 16)

                        def rows(lap, u, d):
                            i, s, lp = item(lap, u, d)
                            if not exists(i, NI):
                                return
                            g, _ = ring(s, lp)
                            off = sp.value_load(items_row[0:1, bass.ds(i * 4, 1)], min_val=0, max_val=OFF_MAX)
                            row = sp.value_load(items_row[0:1, bass.ds(i * 4 + 1, 1)], min_val=0, max_val=NB * P)
                            if after(i, R):
                                hold(sp, sp_passed,
                                     (a_ready, i - R + 1),
                                     (gap_ready, i - R + 1),
                                     (pairs_done, 2 * (i - R + 1)))
                            sp.dma_start(lo_t[:, g, :], low_d[bass.ds(off, IT)].partition_broadcast(P)).then_inc(ld[g], 16)
                            sp.dma_start(pen_t[:, g, :], pen_d[bass.ds(off, IT)].partition_broadcast(P)).then_inc(ld[g], 16)
                            sp.dma_start(fd_t[:, g, :], dst_d[0][bass.ds(row, P), :]).then_inc(ld[g], 16)
                            sp.dma_start(pair_t[:, g, :, :], pair_d[bass.ds(off, IT), :].rearrange("(p j) k -> p j k", j=TJ)).then_inc(ld[g], 16)

                        def step(lap, u):
                            indices(lap, u, 4)
                            rows(lap, u, 0)
                        run_items(sp, step)

                    @block.gpsimd
                    def _(pool):
                        def select(lap, u, d):
                            i, s, _ = item(lap, u, d)
                            if not exists(i, NI):
                                return
                            hold(pool, pool_passed, (pairs_done, 2 * (i + 1)))
                            if after(i, 2):
                                hold(pool, pool_passed, (accp_ready, i - 1))
                            for j in range(SEL_DVE, TJ):
                                nc.gpsimd.tensor_scalar(sel[:, s % 2, j, :], iota_row[:, :], ends_t[:, s, j:j + 1], None,
                                                        ALU.is_equal).then_inc(sel_pool, 1)

                        def gather(lap, u, d):
                            i, s, lp = item(lap, u, d)
                            if not exists(i, NI):
                                return
                            g, _ = ring(s, lp)
                            if after(i, R):
                                hold(pool, pool_passed, (v_ready, i - R + 1))
                            hold(pool, pool_passed, (ldi[s], 16 * (lp + 1)))
                            for j in range(TJ):
                                nc.gpsimd.indirect_dma_start(
                                    out=G[:, g, j, :], out_offset=None, in_=rows_d[0][:, :],
                                    in_offset=bass.IndirectOffsetOnAxis(ap=sidx[s][:, j:j + 1], axis=0)).then_inc(gat[g], 16)

                        def step(lap, u):
                            gather(lap, u, 4)
                            select(lap, u, -1)
                        run_items(pool, step)

                    @block.tensor
                    def _(pe):
                        def front(lap, u, d):
                            i, s, lp = item(lap, u, d)
                            if not exists(i, NI):
                                return
                            b = s % 2
                            g, gl = ring(s, lp)
                            pe.wait_ge(gat[g], 16 * TJ * (gl + 1))
                            pe.wait_ge(ld[g], 64 * (gl + 1))
                            pe.wait_ge(oht_ready, i + 1)
                            if after(i, 2):
                                pe.wait_ge(a_copied, i - 1)
                            av = A[b][:, :].rearrange("p (e j) -> p j e", j=TJ)
                            for j in range(TJ):
                                nc.tensor.matmul(av[:, j, :], G[:, g, j, 0:C], ident[:, :], is_transpose=True,
                                                 start=(j == 0), stop=False, skip_group_check=True)
                            for k in range(3):
                                last = nc.tensor.matmul(A[b][:, :], fd_t[:, g, k * C:(k + 1) * C], oht[:, g, :],
                                                        start=False, stop=(k == 2), skip_group_check=True)
                            last.then_inc(a_ready, 1)

                        def values(lap, u, d):
                            i, s, lp = item(lap, u, d)
                            if not exists(i, NI):
                                return
                            g, gl = ring(s, lp)
                            vv = V[s % 2][:, :].rearrange("p (e j) -> p j e", j=TJ)
                            pe.wait_ge(gat[g], 16 * TJ * (gl + 1))
                            if after(i, 2):
                                pe.wait_ge(wv_ready, i - 1)
                            for j in range(TJ):
                                last = nc.tensor.matmul(vv[:, j, :], G[:, g, j, C:2 * C], ident[:, :], is_transpose=True,
                                                        start=(j == 0), stop=(j == TJ - 1), skip_group_check=True)
                            last.then_inc(v_ready, 1)

                        def turn(lap, u, d):
                            i, s, _ = item(lap, u, d)
                            if not exists(i, NI):
                                return
                            b = s % 2
                            pe.wait_ge(s_ready, i + 1)
                            pe.wait_ge(r_ready, i + 1)
                            if after(i, 1):
                                pe.wait_ge(sre_ready, 2 * i)
                            for j in range(TJ):
                                for k, t in enumerate((s_t, r_t)):
                                    tv = t[:, b, :].rearrange("p (e j) -> p j e", j=TJ)
                                    last = nc.tensor.matmul(sr_p[j // 2][:, j % 2, k * C:(k + 1) * C], tv[:, j, :],
                                                            ident[:, :], is_transpose=True,
                                                            start=(j % 2 == 0 and k == 0), stop=(j % 2 == 1 and k == 1),
                                                            skip_group_check=True)
                                if j % 2:
                                    last.then_inc(srt_ready, 1)

                        def collect(lap, u, d):
                            i, s, _ = item(lap, u, d)
                            if not exists(i, NI):
                                return
                            b = s % 2
                            pe.wait_ge(sel_dve, i + 1)
                            pe.wait_ge(sel_pool, (TJ - SEL_DVE) * (i + 1))
                            pe.wait_ge(sre_ready, 2 * (i + 1))
                            if after(i, 1):
                                pe.wait_ge(acc_done, i)
                            for j in range(TJ):
                                last = nc.tensor.matmul(accp[:, :], sel[:, b, j, :], sr_e[:, b, j, :],
                                                        start=(j == 0), stop=(j == TJ - 1))
                            last.then_inc(accp_ready, 1)

                        def step(lap, u):
                            front(lap, u, 2)
                            turn(lap, u, -1)
                            collect(lap, u, -2)
                            values(lap, u, 1)
                        run_items(pe, step)

                    @block.scalar
                    def _(act):
                        act.wait_ge(zeroed, 5)

                        def bring(lap, u, d):
                            i, s, _ = item(lap, u, d)
                            if not exists(i, NI):
                                return
                            act.wait_ge(a_ready, i + 1)
                            if after(i, R):
                                act.wait_ge(gap_ready, i - R + 2)
                            nc.scalar.activation(e_t[:, s % R, 1:IT + 1], A[s % 2][:, :], ACT.Copy).then_inc(a_copied, 1)

                        def exps(lap, u, d):
                            i, s, _ = item(lap, u, d)
                            if not exists(i, NI):
                                return
                            b = s % 2
                            act.wait_ge(gap_ready, i + 1)
                            if after(i, 2):
                                act.wait_ge(r_ready, i - 1)
                                act.wait_ge(s_ready, i - 1)
                            nc.scalar.activation(c_t[:, b, :], w_t[:, b, :], ACT.Relu).then_inc(up_ready, 1)
                            act.wait_ge(up_ready, i + 1)
                            nc.scalar.activation(w_t[:, b, :], w_t[:, b, :], ACT.Relu, scale=-1.0).then_inc(down_ready, 1)
                            nc.scalar.activation(c_t[:, b, :], c_t[:, b, :], ACT.Exp, scale=-1.0).then_inc(c_ready, 1)
                            act.wait_ge(down_ready, i + 1)
                            nc.scalar.activation(w_t[:, b, :], w_t[:, b, :], ACT.Exp, scale=-1.0).then_inc(w_ready, 1)

                        def evacuate(lap, u, d):
                            i, s, _ = item(lap, u, d)
                            if not exists(i, NI):
                                return
                            b = s % 2
                            if after(i, 2):
                                act.wait_ge(accp_ready, i - 1)
                            for k in range(2):
                                act.wait_ge(srt_ready, 2 * i + k + 1)
                                nc.scalar.activation(sr_e[:, b, 2 * k:2 * k + 2, :], sr_p[k][:, :, :],
                                                     ACT.Copy).then_inc(sre_ready, 1)

                        def step(lap, u):
                            bring(lap, u, 2)
                            evacuate(lap, u, -1)
                            exps(lap, u, 1)
                        run_items(act, step)

                    @block.vector
                    def _(dve):
                        for t in (acc0, e_t[:, :, :], q_t[:, :, :], s_t[:, :, :], r_t[:, :, :]):
                            nc.vector.memset(t, 0.0).then_inc(zeroed, 1)
                        dve.wait_ge(zeroed, 5)

                        def onehot(lap, u, d):
                            i, s, lp = item(lap, u, d)
                            if not exists(i, NI):
                                return
                            g, gl = ring(s, lp)
                            dve.wait_ge(ld[g], 64 * (gl + 1))
                            if after(i, R):
                                dve.wait_ge(a_ready, i - R + 1)
                            if after(i, U):
                                dve.wait_ge(sel_pool, (TJ - SEL_DVE) * (i - U + 1))
                                dve.wait_ge(sel_dve, i - U + 1)
                            nc.vector.tensor_scalar(oht[:, g, :], lo_t[:, g, :], iota_col[:, 0:1], None,
                                                    ALU.is_equal).then_inc(oht_ready, 1)
                            mine = base_bc[:, bass.ds(i, 1)].to_broadcast([P, TJ])
                            nc.vector.tensor_tensor(local[:, bass.ds(i * TJ, TJ)], pair_t[:, g, :, 0], mine,
                                                    ALU.subtract).then_inc(pairs_done, 1)
                            nc.vector.tensor_tensor(ends_t[:, s, :], pair_t[:, g, :, 1], mine,
                                                    ALU.subtract).then_inc(pairs_done, 1)

                        def maximum(lap, u, d):
                            i, s, lp = item(lap, u, d)
                            if not exists(i, NI):
                                return
                            b = s % 2
                            g, gl = ring(s, lp)
                            e = e_t[:, g, 1:IT + 1]
                            dve.wait_ge(a_copied, i + 1)
                            nc.vector.scalar_tensor_tensor(out=e, in0=e, scalar=SLOPE, in1=e,
                                                           op0=ALU.mult, op1=ALU.max).then_inc(e_ready, 1)
                            if after(i, 1):
                                dve.wait_ge(gap_ready, i)
                            nc.vector.tensor_copy(e_t[:, g, 0:1], e_t[:, (g - 1) % R, IT:IT + 1]).then_inc(carry_ready, 1)
                            dve.wait_ge(ld[g], 64 * (gl + 1))
                            dve.wait_ge(e_ready, i + 1)
                            dve.wait_ge(carry_ready, i + 1)
                            nc.vector.tensor_tensor_scan(q_t[:, b, :], e_t[:, g, 0:IT], pen_t[:, g, :],
                                                         q_t[:, 1 - b, IT - 1:IT], ALU.max, ALU.add).then_inc(q_ready, 1)
                            dve.wait_ge(q_ready, i + 1)
                            if after(i, 2):
                                dve.wait_ge(s_ready, i - 1)
                                dve.wait_ge(wv_ready, i - 1)
                            nc.vector.tensor_tensor(w_t[:, b, :], e, q_t[:, b, :], ALU.subtract).then_inc(gap_ready, 1)

                        def sums(lap, u, d):
                            i, s, _ = item(lap, u, d)
                            if not exists(i, NI):
                                return
                            b = s % 2
                            dve.wait_ge(w_ready, i + 1)
                            dve.wait_ge(v_ready, i + 1)
                            if after(i, 2):
                                dve.wait_ge(r_ready, i - 1)
                            nc.vector.tensor_tensor(wv_t[:, b, :], w_t[:, b, :], V[b][:, :], ALU.mult).then_inc(wv_ready, 1)
                            dve.wait_ge(c_ready, i + 1)
                            if after(i, 2):
                                dve.wait_ge(srt_ready, 2 * (i - 1))
                            if after(i, 1):
                                dve.wait_ge(s_ready, i)
                                dve.wait_ge(r_ready, i)
                            nc.vector.tensor_tensor_scan(s_t[:, b, :], c_t[:, b, :], w_t[:, b, :],
                                                         s_t[:, 1 - b, IT - 1:IT], ALU.mult, ALU.add).then_inc(s_ready, 1)
                            dve.wait_ge(wv_ready, i + 1)
                            nc.vector.tensor_tensor_scan(r_t[:, b, :], c_t[:, b, :], wv_t[:, b, :],
                                                         r_t[:, 1 - b, IT - 1:IT], ALU.mult, ALU.add).then_inc(r_ready, 1)

                        def select(lap, u, d):
                            i, s, _ = item(lap, u, d)
                            if not exists(i, NI):
                                return
                            dve.wait_ge(pairs_done, 2 * (i + 1))
                            if after(i, 2):
                                dve.wait_ge(accp_ready, i - 1)
                            nc.vector.tensor_tensor(sel[:, s % 2, 0:SEL_DVE, :],
                                                    iota_row[:, :].unsqueeze(1).to_broadcast([P, SEL_DVE, P]),
                                                    ends_t[:, s, 0:SEL_DVE].unsqueeze(2).to_broadcast([P, SEL_DVE, P]),
                                                    ALU.is_equal).then_inc(sel_dve, 1)

                        def add(lap, u, d):
                            i, s, _ = item(lap, u, d)
                            if not exists(i, NI):
                                return
                            at = dve.value_load(items_row[0:1, bass.ds(i * 4 + 2, 1)], min_val=0, max_val=NB * 2 * C)
                            dve.wait_ge(accp_ready, i + 1)
                            if after(i, 1):
                                dve.wait_ge(acc_done, i)
                            mine = acc0[:, bass.ds(at, 2 * C)]
                            nc.vector.tensor_tensor(mine, mine, accp[:, :], ALU.add).then_inc(acc_done, 1)

                        def step(lap, u):
                            onehot(lap, u, 3)
                            maximum(lap, u, 1)
                            sums(lap, u, 0)
                            select(lap, u, -1)
                            add(lap, u, -3)
                        run_items(dve, step)

        def layer1_edges():
            st = ExitStack()
            with st:
                sidx = [sb(f"l1_sidx{k}", [P, TJ], I32, st) for k in range(U)]
                G = sb("l1_G", [P, R, TJ, 2 * C], F32, st)
                lo_t = sb("l1_lo", [P, R, IT], BF16, st)
                pd_t = sb("l1_pd", [P, R, 3 * C], BF16, st)
                ea_t = sb("l1_ea", [4 * EA, R, IT], BF16, st)
                sh_t = sb("l1_sh", [4 * SH, R, IT], BF16, st)
                oht = sb("l1_oht", [P, R, IT], BF16, st)
                h1_t = sb("l1_h1", [P, 2, IT], F32, st)
                a1_t = sb("l1_a1", [P, 2, IT], F32, st)
                h2_t = sb("l1_h2", [P, 2, IT], F32, st)
                a2_t = sb("l1_a2", [P, 2, IT], F32, st)
                pre_t = sb("l1_pre", [P, 2, TJ, C], F32, st)
                msg_t = sb("l1_msg", [P, R, TJ * C], F32, st)
                w_fc1 = sb("l1_fc1", [4 * EA, 2, C], BF16, st)
                w_aw1 = sb("l1_aw1", [4 * EA, 2, C], BF16, st)
                w_sh_t = sb("l1_wsh", [4 * SH, 2, C], BF16, st)
                small = [sb(f"l1_small{k}", [EA, C], F32, st) for k in range(4)]
                small_cut = [sb(f"l1_small_cut{k}", [EA, 3, C], BF16, st) for k in range(4)]
                small_rest = sb("l1_small_rest", [EA, C], F32, st)
                w_fc2 = sb("l1_fc2", [P, C], F32, st)
                w_aw2 = sb("l1_aw2", [P, C], F32, st)
                w_fc3 = sb("l1_fc3", [P, C], F32, st)
                w_aw3 = sb("l1_aw3", [P, HEADS], F32, st)
                cols = sb("l1_cols", [P, 4], F32, st)
                ab3_bc = sb("l1_ab3", [P, HEADS], F32, st)
                b3_3 = sb("l1_b3", [3, TJ, C], BF16, st)
                ones3 = sb("l1_ones3", [3, P], BF16, st)
                H1 = ps("l1_H1", [P, IT], F32, st)
                A1 = ps("l1_A1", [P, IT], F32, st)
                H2 = ps("l1_H2", [P, IT], F32, st)
                A2 = ps("l1_A2", [P, IT], F32, st)
                SC = ps("l1_SC", [P, TJ, C], F32, st)
                SP_ = ps("l1_SHP", [P, TJ, C], F32, st)
                LG = ps("l1_LG", [P, TJ, HEADS], F32, st)
                s_w = sem("l1_weights", st)
                s_small = sem("l1_small_loaded", st)
                s_cut = sem("l1_small_cut", st)
                s_placed = sem("l1_small_placed", st)
                CUTS, PLACED = 4 * 4 + 4, 3 * 6 + 3 * TJ
                ldi = [sem(f"l1_ldi{k}", st) for k in range(U)]
                ld = [sem(f"l1_ld{k}", st) for k in range(R)]
                gat = [sem(f"l1_gat{k}", st) for k in range(R)]
                store = [sem(f"l1_store{k}", st) for k in range(R)]
                oht_ready = sem("l1_oht_ready", st)
                h1p = sem("l1_h1_product", st)
                a1p = sem("l1_a1_product", st)
                h2p = sem("l1_h2_product", st)
                a2p = sem("l1_a2_product", st)
                h1s = sem("l1_h1_ready", st)
                a1s = sem("l1_a1_ready", st)
                h2s = sem("l1_h2_ready", st)
                a2s = sem("l1_a2_ready", st)
                sc_ready = sem("l1_sc_ready", st)
                sh_ready = sem("l1_sh_ready", st)
                lg_ready = sem("l1_lg_ready", st)
                t_done = sem("l1_scaled", st)
                pre_ready = sem("l1_pre_ready", st)
                lg_done = sem("l1_lg_done", st)
                msg_ready = sem("l1_msg_ready", st)
                with nc.Block() as block:
                    @block.sync
                    def _(sp):
                        for t, w in ((small[0][:, :], fc1), (small[1][:, :], aw1e), (small[2][0:SH, :], w_sh),
                                     (small[3][0:1, :], b3.rearrange("(k c) -> k c", k=1))):
                            sp.dma_start(t, w).then_inc(s_small, 16)
                        for t, w in ((w_fc2, fc2), (w_aw2, aw2), (w_fc3, fc3), (w_aw3, aw3)):
                            sp.dma_start(t[:, :], w).then_inc(s_w, 16)
                        for k, v in enumerate((b1, ab1, b2, ab2)):
                            sp.dma_start(cols[:, k:k + 1], v.rearrange("(p k) -> p k", k=1)).then_inc(s_w, 16)
                        sp.dma_start(ab3_bc[:, :], ab3.partition_broadcast(P)).then_inc(s_w, 16)
                        sp.wait_ge(s_cut, CUTS)
                        for k, (t, n) in enumerate(((w_fc1, EA), (w_aw1, EA), (w_sh_t, SH))):
                            for half, parts in enumerate(((0, 0, 0), (1, 1, None, 2))):
                                for group, m in enumerate(parts):
                                    if m is not None:
                                        sp.dma_start(t[group * n:(group + 1) * n, half, :],
                                                     small_cut[k][0:n, m, :]).then_inc(s_placed, 16)
                        for k in range(3):
                            for j in range(TJ):
                                sp.dma_start(b3_3[k:k + 1, j, :], small_cut[3][0:1, k, :]).then_inc(s_placed, 16)

                        def indices(lap, u, d):
                            i, s, lp = item(lap, u, d)
                            if not exists(i, NI):
                                return
                            off = sp.value_load(items_row[0:1, bass.ds(i * 4, 1)], min_val=0, max_val=OFF_MAX)
                            g, gl = ring(s, lp)
                            if after(i, U):
                                hold(sp, sp_passed, (gat[g], 16 * TJ * (gl + 1 - U // R)))
                            sp.dma_start(sidx[s][:, :], src_pad[bass.ds(off, IT)].rearrange("(p j) -> p j", j=TJ)).then_inc(ldi[s], 16)

                        def rows(lap, u, d):
                            i, s, lp = item(lap, u, d)
                            if not exists(i, NI):
                                return
                            g, _ = ring(s, lp)
                            off = sp.value_load(items_row[0:1, bass.ds(i * 4, 1)], min_val=0, max_val=OFF_MAX)
                            row = sp.value_load(items_row[0:1, bass.ds(i * 4 + 1, 1)], min_val=0, max_val=NB * P)
                            if after(i, R):
                                hold(sp, sp_passed,
                                     (a1p, i - R + 1),
                                     (h1p, i - R + 1),
                                     (sh_ready, i - R + 1))
                            sp.dma_start(lo_t[:, g, :], low_d[bass.ds(off, IT)].partition_broadcast(P)).then_inc(ld[g], 16)
                            sp.dma_start(pd_t[:, g, :], dst_d[1][bass.ds(row, P), :]).then_inc(ld[g], 16)
                            for t, d, n in ((ea_t, ea_d, EA), (sh_t, sh_d, SH)):
                                sp.dma_start(t[0:3 * n, g, :], d[:, bass.ds(off, IT)]).then_inc(ld[g], 16)
                                sp.dma_start(t[3 * n:4 * n, g, :], d[0:n, bass.ds(off, IT)]).then_inc(ld[g], 16)

                        def step(lap, u):
                            indices(lap, u, 4)
                            rows(lap, u, 0)
                        run_items(sp, step)

                    @block.gpsimd
                    def _(pool):
                        def step(lap, u):
                            i, s, lp = item(lap, u, 4)
                            if not exists(i, NI):
                                return
                            g, _ = ring(s, lp)
                            if after(i, R):
                                hold(pool, pool_passed,
                                     (a1p, i - R + 1),
                                     (t_done, i - R + 1))
                            hold(pool, pool_passed, (ldi[s], 16 * (lp + 1)))
                            for j in range(TJ):
                                nc.gpsimd.indirect_dma_start(
                                    out=G[:, g, j, :], out_offset=None, in_=rows_d[1][:, :],
                                    in_offset=bass.IndirectOffsetOnAxis(ap=sidx[s][:, j:j + 1], axis=0)).then_inc(gat[g], 16)
                        run_items(pool, step)

                    @block.tensor
                    def _(pe):
                        pe.wait_ge(s_w, 16 * 9)
                        pe.wait_ge(s_cut, CUTS)
                        pe.wait_ge(s_placed, 16 * PLACED)

                        def first(lap, u, d):
                            i, s, lp = item(lap, u, d)
                            if not exists(i, NI):
                                return
                            g, gl = ring(s, lp)
                            pe.wait_ge(ld[g], 96 * (gl + 1))
                            if after(i, 1):
                                pe.wait_ge(h1s, i)
                            nc.tensor.matmul(H1[:, :], w_fc1[0:3 * EA, 0, :], ea_t[0:3 * EA, g, :], start=True, stop=False)
                            nc.tensor.matmul(H1[:, :], w_fc1[:, 1, :], ea_t[:, g, :], start=False, stop=True).then_inc(h1p, 1)
                            pe.wait_ge(gat[g], 16 * TJ * (gl + 1))
                            pe.wait_ge(oht_ready, i + 1)
                            if after(i, 1):
                                pe.wait_ge(a1s, i)
                            av = A1[:, :].rearrange("p (e j) -> p j e", j=TJ)
                            for j in range(TJ):
                                nc.tensor.matmul(av[:, j, :], G[:, g, j, C:2 * C], ident[:, :], is_transpose=True,
                                                 start=(j == 0), stop=False, skip_group_check=True)
                            for k in range(3):
                                nc.tensor.matmul(A1[:, :], pd_t[:, g, k * C:(k + 1) * C], oht[:, g, :],
                                                 start=False, stop=False, skip_group_check=True)
                            nc.tensor.matmul(A1[:, :], w_aw1[0:3 * EA, 0, :], ea_t[0:3 * EA, g, :], start=False, stop=False,
                                             skip_group_check=True)
                            nc.tensor.matmul(A1[:, :], w_aw1[:, 1, :], ea_t[:, g, :], start=False, stop=True,
                                             skip_group_check=True).then_inc(a1p, 1)

                        def second(lap, u, d):
                            i, s, _ = item(lap, u, d)
                            if not exists(i, NI):
                                return
                            b = s % 2
                            pe.wait_ge(h1s, i + 1)
                            if after(i, 1):
                                pe.wait_ge(h2s, i)
                            nc.tensor.matmul(H2[:, :], w_fc2[:, :], h1_t[:, b, :], start=True, stop=True).then_inc(h2p, 1)
                            pe.wait_ge(a1s, i + 1)
                            if after(i, 1):
                                pe.wait_ge(a2s, i)
                            nc.tensor.matmul(A2[:, :], w_aw2[:, :], a1_t[:, b, :], start=True, stop=True).then_inc(a2p, 1)

                        def third(lap, u, d):
                            i, s, _ = item(lap, u, d)
                            if not exists(i, NI):
                                return
                            b = s % 2
                            pe.wait_ge(h2s, i + 1)
                            if after(i, 1):
                                pe.wait_ge(t_done, i)
                            nc.tensor.matmul(SC[:, :, :], ones3[:, :], b3_3[:, :, :], start=True, stop=False,
                                             skip_group_check=True)
                            hv = h2_t[:, b, :].rearrange("p (e j) -> p j e", j=TJ)
                            sv = sh_t[:, s % R, :].rearrange("p (e j) -> p j e", j=TJ)
                            a2v = a2_t[:, b, :].rearrange("p (e j) -> p j e", j=TJ)
                            for j in range(TJ):
                                last = nc.tensor.matmul(SC[:, j, :], hv[:, j, :], w_fc3[:, :], start=False,
                                                        stop=(j == TJ - 1), skip_group_check=True)
                            last.then_inc(sc_ready, 1)
                            if after(i, 1):
                                pe.wait_ge(pre_ready, i)
                            for j in range(TJ):
                                nc.tensor.matmul(SP_[:, j, :], sv[0:3 * SH, j, :], w_sh_t[0:3 * SH, 0, :], start=True, stop=False)
                                last = nc.tensor.matmul(SP_[:, j, :], sv[:, j, :], w_sh_t[:, 1, :], start=False, stop=True)
                            last.then_inc(sh_ready, 1)
                            pe.wait_ge(a2s, i + 1)
                            if after(i, 1):
                                pe.wait_ge(lg_done, i)
                            for j in range(TJ):
                                last = nc.tensor.matmul(LG[:, j, :], a2v[:, j, :], w_aw3[:, :], start=True, stop=True)
                            last.then_inc(lg_ready, 1)

                        def step(lap, u):
                            first(lap, u, 2)
                            second(lap, u, 1)
                            third(lap, u, 0)
                        run_items(pe, step)

                    @block.scalar
                    def _(act):
                        act.wait_ge(s_w, 16 * 9)

                        def silu(lap, u, d, product, ready, used, out_t, in_p, col):
                            i, s, _ = item(lap, u, d)
                            if not exists(i, NI):
                                return
                            act.wait_ge(product, i + 1)
                            if after(i, 2):
                                act.wait_ge(used, i - 1)
                            nc.scalar.activation(out_t[:, s % 2, :], in_p[:, :], ACT.Silu,
                                                 bias=cols[:, col:col + 1]).then_inc(ready, 1)

                        def message(lap, u, d):
                            i, s, lp = item(lap, u, d)
                            if not exists(i, NI):
                                return
                            act.wait_ge(pre_ready, i + 1)
                            g, gl = ring(s, lp)
                            if after(i, R):
                                act.wait_ge(store[g], 16 * gl)
                            nc.scalar.activation(msg_t[:, g, :], pre_t[:, s % 2, :, :].rearrange("p j c -> p (j c)"),
                                                 ACT.Silu).then_inc(msg_ready, 1)

                        def keep(lap, u, d):
                            i, s, _ = item(lap, u, d)
                            if not exists(i, NI):
                                return
                            act.wait_ge(msg_ready, i + 1)
                            act.dma_start(msg_d[bass.ds(i, 1), :, :].rearrange("a p c -> (a p) c"),
                                          msg_t[:, s % R, :]).then_inc(store[s % R], 16)

                        def step(lap, u):
                            silu(lap, u, 2, h1p, h1s, h2p, h1_t, H1, 0)
                            silu(lap, u, 2, a1p, a1s, a2p, a1_t, A1, 1)
                            silu(lap, u, 1, h2p, h2s, sc_ready, h2_t, H2, 2)
                            silu(lap, u, 1, a2p, a2s, lg_ready, a2_t, A2, 3)
                            message(lap, u, -1)
                            keep(lap, u, -2)
                        run_items(act, step)
                        for k in range(R):
                            act.wait_ge(store[k], 16 * (NI // R))

                    @block.vector
                    def _(dve):
                        done = 0

                        def link(ins):
                            nonlocal done
                            done += 1
                            ins.then_inc(s_cut, 1)
                            dve.wait_ge(s_cut, done)
                        link(nc.vector.memset(ones3[:, :], 1.0))
                        for t in (w_fc1, w_aw1, w_sh_t):
                            link(nc.vector.memset(t[:, :, :], 0.0))
                        dve.wait_ge(s_small, 64)
                        for k, n in enumerate((EA, EA, SH, 1)):
                            v, cut, rest = small[k][0:n, :], small_cut[k], small_rest[0:n, :]
                            link(nc.vector.tensor_copy(cut[0:n, 0, :], v))
                            link(nc.vector.tensor_tensor(rest, v, cut[0:n, 0, :], ALU.subtract))
                            link(nc.vector.tensor_copy(cut[0:n, 1, :], rest))
                            link(nc.vector.tensor_tensor(cut[0:n, 2, :], rest, cut[0:n, 1, :], ALU.subtract))
                        dve.wait_ge(s_w, 16 * 9)

                        def onehot(lap, u, d):
                            i, s, lp = item(lap, u, d)
                            if not exists(i, NI):
                                return
                            g, gl = ring(s, lp)
                            dve.wait_ge(ld[g], 96 * (gl + 1))
                            if after(i, R):
                                dve.wait_ge(a1p, i - R + 1)
                            nc.vector.tensor_scalar(oht[:, g, :], lo_t[:, g, :], iota_col[:, 0:1], None,
                                                    ALU.is_equal).then_inc(oht_ready, 1)

                        def message(lap, u, d):
                            i, s, lp = item(lap, u, d)
                            if not exists(i, NI):
                                return
                            b = s % 2
                            g, gl = ring(s, lp)
                            dve.wait_ge(gat[g], 16 * TJ * (gl + 1))
                            dve.wait_ge(sc_ready, i + 1)
                            if after(i, 2):
                                dve.wait_ge(msg_ready, i - 1)
                            nc.vector.tensor_tensor(pre_t[:, b, :, :], G[:, g, :, 0:C], SC[:, :, :], ALU.mult).then_inc(t_done, 1)
                            dve.wait_ge(t_done, i + 1)
                            dve.wait_ge(sh_ready, i + 1)
                            nc.vector.tensor_tensor(pre_t[:, b, :, :], pre_t[:, b, :, :], SP_[:, :, :], ALU.add).then_inc(pre_ready, 1)
                            dve.wait_ge(lg_ready, i + 1)
                            mine = logits[:, bass.ds(i * (TJ * HEADS), TJ * HEADS)].rearrange("p (j h) -> p j h", h=HEADS)
                            nc.vector.tensor_tensor(mine, LG[:, :, :], ab3_bc[:, :].unsqueeze(1).to_broadcast([P, TJ, HEADS]),
                                                    ALU.add).then_inc(lg_done, 1)

                        def step(lap, u):
                            onehot(lap, u, 3)
                            message(lap, u, 0)
                        run_items(dve, step)

        def layer1_aggregate():
            T = NI * TJ
            st = ExitStack()
            with st:
                bad = sb("ag_bad", [P, T], F32, st)
                late = sb("ag_late", [P, T], F32, st)
                ex = sb("ag_ex", [P, HEADS, T], F32, st)
                alpha = sb("ag_alpha", [P, 2, T], F32, st)
                mx = sb("ag_mx", [P, HEADS], F32, st)
                mx_all = sb("ag_mx_all", [P, HEADS], F32, st)
                neg = sb("ag_neg", [P, HEADS], F32, st)
                tot = sb("ag_tot", [P, HEADS], F32, st)
                tot_all = sb("ag_tot_all", [P, HEADS], F32, st)
                share = sb("ag_share", [P, HEADS], F32, st)
                msg_t = sb("ag_msg", [P, R, TJ, C], F32, st)
                pick = sb("ag_pick", [P, 2, TJ, P], F32, st)
                accp = [ps(f"ag_accp{k}", [P, C], F32, st) for k in range(2)]
                s_chain = sem("ag_chain", st)
                s_mx = sem("ag_mx_ready", st)
                s_mxa = sem("ag_mx_all_ready", st)
                s_neg = sem("ag_neg_ready", st)
                s_ex = sem("ag_ex_ready", st)
                s_tot = sem("ag_tot_ready", st)
                ld = [sem(f"ag_ld{k}", st) for k in range(R)]
                pick_ready = sem("ag_pick_ready", st)
                accp_ready = sem("ag_accp_ready", st)
                acc_done = sem("ag_acc_done", st)
                with nc.Block() as block:
                    @block.sync
                    def _(sp):
                        def step(lap, u):
                            i, s, lp = item(lap, u)
                            if not exists(i, NI):
                                return
                            if after(i, R):
                                hold(sp, sp_passed, (accp_ready, i - R + 1))
                            sp.dma_start(msg_t[:, s % R, :, :], msg_d[bass.ds(i, 1), :, :].rearrange(
                                "a p (j c) -> (a p) j c", j=TJ)).then_inc(ld[s % R], 16)
                        run_items(sp, step)

                    @block.gpsimd
                    def _(pool):
                        pool.wait_ge(s_mx, 1)
                        nc.gpsimd.partition_all_reduce(mx_all[:, :], mx[:, :], P, RMAX).then_inc(s_mxa, 1)
                        pool.wait_ge(s_ex, HEADS)
                        nc.gpsimd.partition_all_reduce(tot_all[:, :], tot[:, :], P, RADD).then_inc(s_tot, 1)

                    @block.scalar
                    def _(act):
                        lg = logits.rearrange("p (t h) -> p h t", h=HEADS)
                        act.wait_ge(s_neg, 1)
                        for h in range(HEADS):
                            nc.scalar.activation(ex[:, h, :], lg[:, h, :], ACT.Exp, bias=neg[:, h:h + 1],
                                                 accum_out=tot[:, h:h + 1]).then_inc(s_ex, 1)

                    @block.tensor
                    def _(pe):
                        def step(lap, u):
                            i, s, lp = item(lap, u)
                            if not exists(i, NI):
                                return
                            b = s % 2
                            g, gl = ring(s, lp)
                            pe.wait_ge(ld[g], 16 * (gl + 1))
                            pe.wait_ge(pick_ready, TJ * (i + 1))
                            if after(i, 2):
                                pe.wait_ge(acc_done, i - 1)
                            for j in range(TJ):
                                last = nc.tensor.matmul(accp[b][:, :], pick[:, b, j, :], msg_t[:, g, j, :],
                                                        start=(j == 0), stop=(j == TJ - 1))
                            last.then_inc(accp_ready, 1)
                        run_items(pe, step)

                    @block.vector
                    def _(dve):
                        chain = [0]

                        def link(ins):
                            chain[0] += 1
                            ins.then_inc(s_chain, 1)
                            dve.wait_ge(s_chain, chain[0])
                        link(nc.vector.tensor_scalar(bad[:, :], local[:, :], 0.0, None, ALU.is_lt))
                        link(nc.vector.scalar_tensor_tensor(out=late[:, :], in0=local[:, :], scalar=float(P), in1=bad[:, :],
                                                            op0=ALU.is_ge, op1=ALU.add))
                        link(nc.vector.tensor_scalar(bad[:, :], late[:, :], FAR, None, ALU.mult))
                        lv = logits.rearrange("p (t h) -> p t h", h=HEADS)
                        link(nc.vector.tensor_tensor(lv, lv, bad[:, :].unsqueeze(2).to_broadcast([P, T, HEADS]), ALU.add))
                        nc.vector.tensor_reduce(mx[:, :], logits.rearrange("p (t h) -> p h t", h=HEADS), AX_X,
                                                ALU.max).then_inc(s_mx, 1)
                        dve.wait_ge(s_mxa, 1)
                        nc.vector.tensor_scalar(neg[:, :], mx_all[:, :], -1.0, None, ALU.mult).then_inc(s_neg, 1)
                        dve.wait_ge(s_tot, 1)
                        link(nc.vector.tensor_scalar(share[:, :], tot_all[:, :], float(HEADS), None, ALU.mult))
                        link(nc.vector.reciprocal(share[:, :], share[:, :]))
                        link(nc.vector.tensor_scalar(alpha[:, 0, :], ex[:, 0, :], share[:, 0:1], None, ALU.mult))
                        for h in range(1, HEADS):
                            link(nc.vector.scalar_tensor_tensor(out=alpha[:, h % 2, :], in0=ex[:, h, :],
                                                                scalar=share[:, h:h + 1], in1=alpha[:, (h - 1) % 2, :],
                                                                op0=ALU.mult, op1=ALU.add))
                        al = alpha[:, (HEADS - 1) % 2, :]
                        link(nc.vector.memset(acc1, 0.0))

                        def weigh(lap, u, d):
                            i, s, _ = item(lap, u, d)
                            if not exists(i, NI):
                                return
                            b = s % 2
                            if after(i, 2):
                                dve.wait_ge(accp_ready, i - 1)
                            for j in range(TJ):
                                nc.vector.tensor_scalar(pick[:, b, j, :], iota_row[:, :], local[:, bass.ds(i * TJ + j, 1)],
                                                        al[:, bass.ds(i * TJ + j, 1)], ALU.is_equal,
                                                        ALU.mult).then_inc(pick_ready, 1)

                        def add(lap, u, d):
                            i, s, _ = item(lap, u, d)
                            if not exists(i, NI):
                                return
                            at = dve.value_load(items_row[0:1, bass.ds(i * 4 + 1, 1)], min_val=0, max_val=NB * P)
                            dve.wait_ge(accp_ready, i + 1)
                            if after(i, 1):
                                dve.wait_ge(acc_done, i)
                            mine = acc1[:, bass.ds(at, C)]
                            nc.vector.tensor_tensor(mine, mine, accp[s % 2][:, :], ALU.add).then_inc(acc_done, 1)

                        def step(lap, u):
                            weigh(lap, u, 1)
                            add(lap, u, 0)
                        run_items(dve, step)

        def finish():
            st = ExitStack()
            with st:
                w_o = sb("fi_w", [P, C], F32, st)
                a_b = sb("fi_ab", [P, 2, C], F32, st)
                a_t = sb("fi_at", [P, 2, C], F32, st)
                stats = sb("fi_stats", [P, 3, NBT], F32, st)
                O = sb("fi_O", [P, NBT, C], F32, st)
                tp = [ps(f"fi_tp{k}", [P, C], F32, st) for k in range(2)]
                pp = [ps(f"fi_pp{k}", [P, C], F32, st) for k in range(2)]
                s_in = sem("fi_in", st)
                s_chain = sem("fi_chain", st)
                s_var = sem("fi_var", st)
                s_root = sem("fi_root", st)
                s_tp = sem("fi_tp_ready", st)
                s_ab = sem("fi_ab_ready", st)
                s_at = sem("fi_at_ready", st)
                s_pp = sem("fi_pp_ready", st)
                s_sum = sem("fi_sum", st)
                s_fin = sem("fi_fin", st)
                s_out = sem("fi_out", st)
                with nc.Block() as block:
                    @block.sync
                    def _(sp):
                        sp.dma_start(w_o[:, :], w_out).then_inc(s_in, 16)
                        sp.wait_ge(s_fin, 1)
                        full = N // P
                        sp.dma_start(out[0:full * P, :].rearrange("(n p) c -> p n c", p=P), O[:, 0:full, :]).then_inc(s_out, 16)
                        sp.dma_start(out[full * P:N, :], O[0:N - full * P, full, :]).then_inc(s_out, 16)
                        sp.wait_ge(s_out, 32)

                    @block.tensor
                    def _(pe):
                        pe.wait_ge(s_in, 16)

                        def step(lap, u):
                            i, s, _ = item(lap, u, 1, 2)
                            if exists(i, NBT):
                                if after(i, 2):
                                    pe.wait_ge(s_at, i - 1)
                                pe.wait_ge(s_ab, i + 1)
                                nc.tensor.transpose(tp[s][:, :], a_b[:, s, :], ident[:, :]).then_inc(s_tp, 1)
                            i, s, _ = item(lap, u, 0, 2)
                            if exists(i, NBT):
                                pe.wait_ge(s_at, i + 1)
                                if after(i, 2):
                                    pe.wait_ge(s_sum, i - 1)
                                nc.tensor.matmul(pp[s][:, :], a_t[:, s, :], w_o[:, :], start=True, stop=True).then_inc(s_pp, 1)
                        run_items(pe, step, NBT // 2, 2)

                    @block.gpsimd
                    def _(pool):
                        def step(lap, u):
                            i, s, _ = item(lap, u, 0, 2)
                            if not exists(i, NBT):
                                return
                            if after(i, 2):
                                pool.wait_ge(s_tp, i - 1)
                            nc.gpsimd.tensor_copy(a_b[:, s, :], acc1[:, bass.ds(i * C, C)]).then_inc(s_ab, 1)
                        run_items(pool, step, NBT // 2, 2)

                    @block.scalar
                    def _(act):
                        def step(lap, u):
                            i, s, _ = item(lap, u, 0, 2)
                            if not exists(i, NBT):
                                return
                            act.wait_ge(s_tp, i + 1)
                            if after(i, 2):
                                act.wait_ge(s_pp, i - 1)
                            nc.scalar.activation(a_t[:, s, :], tp[s][:, :], ACT.Copy).then_inc(s_at, 1)
                        run_items(act, step, NBT // 2, 2)
                        norm_scalar(act, stats, s_var, s_root)

                    @block.vector
                    def _(dve):
                        def step(lap, u):
                            i, s, _ = item(lap, u, 0, 2)
                            if not exists(i, NBT):
                                return
                            dve.wait_ge(s_pp, i + 1)
                            mine = H[:, bass.ds(i, 1), :].rearrange("p n c -> p (n c)")
                            nc.vector.tensor_tensor(mine, mine, pp[s][:, :], ALU.add).then_inc(s_sum, 1)
                        run_items(dve, step, NBT // 2, 2)
                        dve.wait_ge(s_sum, NBT)
                        norm_vector(dve, [s_chain, 0], H[:, :, :], s_var, s_root, stats, O[:, :, :], False)
                        nc.vector.tensor_tensor(O[:, :, :], O[:, :, :], X[:, :, :], ALU.add).then_inc(s_fin, 1)

        index_pass()
        split_attributes()
        node_tables(0, w0cat, b0cat)
        layer0_edges()
        node_tables(1, w1cat, None)
        layer1_edges()
        layer1_aggregate()
        finish()


def kernel(x, src, dst, edge_attr_16, edge_attr_32, L0_gnn_W_src, L0_gnn_b_src, L0_gnn_W_dst, L0_gnn_b_dst,
           L0_gnn_W_v, L0_gnn_b_v, L1_gnn_W_node, L1_gnn_fc1, L1_gnn_b1, L1_gnn_fc2, L1_gnn_b2, L1_gnn_fc3,
           L1_gnn_b3, L1_gnn_W_sh, L1_gnn_aW1, L1_gnn_ab1, L1_gnn_aW2, L1_gnn_ab2, L1_gnn_aW3, L1_gnn_ab3,
           L1_gnn_W_out):
    import numpy as np
    import concourse.bacc as bacc
    from concourse.bass_utils import run_bass_kernel_spmd

    def pad(a, shape, at, fill=0):
        a = np.asarray(a)
        full = np.full(shape, fill, a.dtype)
        full[tuple(slice(o, o + n) for o, n in zip(at, a.shape))] = a
        return full
    aW1 = np.asarray(L1_gnn_aW1)
    half = C // 2
    dst_pad = pad(dst, (EP + 2,), (1,), NO_NODE)
    dst_pad[0] = -1
    laid = {
        "x": pad(x, (NP, C), (0, 0)),
        "src_pad": pad(src, (EP,), (0,)),
        "dst_pad": dst_pad,
        "ea32": pad(np.asarray(edge_attr_32).T, (EA, EP), (0, 0)),
        "ea16": pad(np.asarray(edge_attr_16).T, (SH, EP), (0, 0)),
        "w0cat": np.concatenate([np.asarray(w).T for w in (L0_gnn_W_src, L0_gnn_W_v, L0_gnn_W_dst)], axis=1),
        "b0cat": np.concatenate([np.asarray(b) for b in (L0_gnn_b_src, L0_gnn_b_v, L0_gnn_b_dst)]),
        "w1cat": np.concatenate([np.asarray(L1_gnn_W_node), pad(aW1[0:half], (C, C), (0, 0)),
                                 pad(aW1[half:2 * half], (C, C), (0, 0))], axis=1),
        "fc1": L1_gnn_fc1, "b1": L1_gnn_b1, "fc2": L1_gnn_fc2, "b2": L1_gnn_b2, "fc3": L1_gnn_fc3,
        "b3": L1_gnn_b3, "w_sh": L1_gnn_W_sh, "aw1e": aW1[2 * half:], "ab1": L1_gnn_ab1, "aw2": L1_gnn_aW2,
        "ab2": L1_gnn_ab2, "aw3": L1_gnn_aW3, "ab3": L1_gnn_ab3, "w_out": L1_gnn_W_out,
    }
    nc = bacc.Bacc("TRN2", target_bir_lowering=False, num_devices=1)
    arrays, args = {}, []
    for name, a in laid.items():
        a = np.ascontiguousarray(a)
        arrays[f"in_{name}_dram"] = a
        args.append(nc.dram_tensor(f"in_{name}_dram", a.shape, mybir.dt.from_np(a.dtype), kind="ExternalInput").ap())
    args.append(nc.dram_tensor("out_dram", (N, C), F32, kind="ExternalOutput").ap())
    build(nc, *args)
    r = run_bass_kernel_spmd(nc, [arrays], core_ids=[0])
    return r.results[0]["out_dram"]
```
